# Optimizing a Trainium2 kernel written in Bass

```python
import numpy as np
import jax
import jax.numpy as jnp

def _softmax(x, axis=-1):
    return jax.nn.softmax(x, axis=axis)

def _gelu(x):
    return jax.nn.gelu(x, approximate=True)

def _silu(x):
    return jax.nn.silu(x)

def _sigmoid(x):
    return jax.nn.sigmoid(x)

def _layernorm(x, axis=-1, eps=1e-05):
    m = jnp.mean(x, axis=axis, keepdims=True)
    v = jnp.var(x, axis=axis, keepdims=True)
    return (x - m) / jnp.sqrt(v + eps)

def _scatter_add(tgt, idx, src, axis=0):
    return tgt.at[idx].add(src)

def _segment_sum(src, seg, n):
    return jax.ops.segment_sum(src, seg, n)
kernel_name = 'mk_decoder_preln_d1_seqx_r8_b62300'

def setup_inputs(seed: int=0):
    np.random.seed(seed)
    _w = jnp.asarray

    def _rec_inputs():
        import jax
        import jax.numpy as jnp
        _rk = jax.random.key(seed)
        x = 7.22e-05 + 1 * jax.random.normal(jax.random.fold_in(_rk, 1), (4, 256, 256), jnp.float32)
        _lenS = 256 - jax.random.randint(jax.random.fold_in(_rk, 7), (4,), 0, max(1, 256 // 4) + 1, jnp.int32)
        _lenS2 = 256 - jax.random.randint(jax.random.fold_in(_rk, 8), (4,), 0, max(1, 256 // 4) + 1, jnp.int32)
        _ctx_512P = jax.random.normal(jax.random.fold_in(_rk, 11), (4, 16, 64), jnp.float32)
        _ctx_512c = jax.random.dirichlet(jax.random.fold_in(_rk, 511), 0.3 * jnp.ones((16,), jnp.float32), (4, 256))
        _ctx_512t = jnp.einsum('bsk,bkd->bsd', _ctx_512c, _ctx_512P)
        _ctx_512t = _ctx_512t * jax.lax.rsqrt(jnp.mean(jnp.square(_ctx_512t)) + 1e-12) * 0.953939
        ctx_512 = -0.000514642 + 1.00011 * (_ctx_512t + 0.3 * jax.random.normal(jax.random.fold_in(_rk, 611), (4, 256, 64), jnp.float32))
        return (x, ctx_512)
    x, ctx_512 = _rec_inputs()

    def _L0_attn_setup():
        import jax, jax.numpy as jnp
        import numpy as np
        B, S, E = (2, 256, 256)
        H, G = (32, 8)
        D = E // H
        key = jax.random.key(seed)
        ks = jax.random.split(key, 5)
        scale = 1.0 / np.sqrt(E)
        return {'X': jax.random.normal(ks[0], (B, S, E), dtype=jnp.float32), 'Wq': jax.random.normal(ks[1], (E, E), dtype=jnp.float32) * scale, 'Wk': jax.random.normal(ks[2], (E, G * D), dtype=jnp.float32) * scale, 'Wv': jax.random.normal(ks[3], (E, G * D), dtype=jnp.float32) * scale, 'Wo': jax.random.normal(ks[4], (E, E), dtype=jnp.float32) * scale}
    _L0_attn_all = _L0_attn_setup()
    _L0_attn_in = {k: v for k, v in _L0_attn_all.items() if k in ('Wq', 'Wk', 'Wv', 'Wo')}
    del _L0_attn_all

    def _L0_xattn_setup():
        import jax, jax.numpy as jnp
        import numpy as np
        B, S, H, NH, L = (2, 256, 256, 16, 64)
        HD = H // NH
        key = jax.random.key(seed)
        k1, k2, k3, k4, k5 = jax.random.split(key, 5)
        scale = 0.02
        return {'q': jax.random.normal(k1, (B, S, H), dtype=jnp.float32), 'latent_kv': jax.random.normal(k2, (B, S, L), dtype=jnp.float32), 'Wq': jax.random.normal(k3, (H, H), dtype=jnp.float32) * scale, 'Wkv_expand': jax.random.normal(k4, (2 * H, L), dtype=jnp.float32) * scale, 'Wout': jax.random.normal(k5, (H, H), dtype=jnp.float32) * scale}
    _L0_xattn_all = _L0_xattn_setup()
    _L0_xattn_in = {k: v for k, v in _L0_xattn_all.items() if k in ('Wq', 'Wkv_expand', 'Wout')}
    del _L0_xattn_all

    def _L0_ffn_setup():
        import jax, jax.numpy as jnp
        import numpy as np
        NUM_EXPERTS = 8
        TOP_K = 2
        ROUTED_SCALE = 1.0
        D_MODEL = 256
        D_FFN = 176
        key = jax.random.key(seed)
        ks = jax.random.split(key, 8)
        s = 0.02
        return {'hidden_states': jax.random.normal(ks[0], (2, 128, D_MODEL), jnp.float32), 'gate_w': jax.random.normal(ks[1], (NUM_EXPERTS, D_MODEL), jnp.float32) * s, 'w_gate': jax.random.normal(ks[2], (NUM_EXPERTS, D_MODEL, D_FFN), jnp.float32) * s, 'w_up': jax.random.normal(ks[3], (NUM_EXPERTS, D_MODEL, D_FFN), jnp.float32) * s, 'w_down': jax.random.normal(ks[4], (NUM_EXPERTS, D_FFN, D_MODEL), jnp.float32) * s, 'sw_gate': jax.random.normal(ks[5], (D_MODEL, D_FFN), jnp.float32) * s, 'sw_up': jax.random.normal(ks[6], (D_MODEL, D_FFN), jnp.float32) * s, 'sw_down': jax.random.normal(ks[7], (D_FFN, D_MODEL), jnp.float32) * s}
    _L0_ffn_all = _L0_ffn_setup()
    _L0_ffn_in = {k: v for k, v in _L0_ffn_all.items() if k in ('gate_w', 'w_gate', 'w_up', 'w_down', 'sw_gate', 'sw_up', 'sw_down')}
    del _L0_ffn_all
    return {'x': x, 'ctx_512': ctx_512, 'L0_attn_Wq': _L0_attn_in['Wq'], 'L0_attn_Wk': _L0_attn_in['Wk'], 'L0_attn_Wv': _L0_attn_in['Wv'], 'L0_attn_Wo': _L0_attn_in['Wo'], 'L0_xattn_Wq': _L0_xattn_in['Wq'], 'L0_xattn_Wkv_expand': _L0_xattn_in['Wkv_expand'], 'L0_xattn_Wout': _L0_xattn_in['Wout'], 'L0_ffn_gate_w': _L0_ffn_in['gate_w'], 'L0_ffn_w_gate': _L0_ffn_in['w_gate'], 'L0_ffn_w_up': _L0_ffn_in['w_up'], 'L0_ffn_w_down': _L0_ffn_in['w_down'], 'L0_ffn_sw_gate': _L0_ffn_in['sw_gate'], 'L0_ffn_sw_up': _L0_ffn_in['sw_up'], 'L0_ffn_sw_down': _L0_ffn_in['sw_down']}

def reference(x, ctx_512, L0_attn_Wq, L0_attn_Wk, L0_attn_Wv, L0_attn_Wo, L0_xattn_Wq, L0_xattn_Wkv_expand, L0_xattn_Wout, L0_ffn_gate_w, L0_ffn_w_gate, L0_ffn_w_up, L0_ffn_w_down, L0_ffn_sw_gate, L0_ffn_sw_up, L0_ffn_sw_down):
    import jax
    import jax.numpy as jnp

    def _L0_attn_ref(X, Wq, Wk, Wv, Wo):
        import jax, jax.numpy as jnp
        import numpy as np
        B, S, E = (2, 256, 256)
        H, G = (32, 8)
        D = E // H
        b, s, e = X.shape
        q = (X @ Wq).reshape(b, s, H, D).transpose(0, 2, 1, 3)
        k = (X @ Wk).reshape(b, s, G, D).transpose(0, 2, 1, 3)
        v = (X @ Wv).reshape(b, s, G, D).transpose(0, 2, 1, 3)
        q = q.reshape(b, H // G, G, s, D)
        scores = jnp.einsum('bagsd,bgtd->bagst', q, k) / np.sqrt(D)
        causal = jnp.tril(jnp.ones((s, s), dtype=bool))
        scores = jnp.where(causal, scores, -jnp.inf)
        probs = jax.nn.softmax(scores, axis=-1)
        out = jnp.einsum('bagst,bgtd->bagsd', probs, v)
        out = out.reshape(b, H, s, D).transpose(0, 2, 1, 3).reshape(b, s, e)
        return out @ Wo

    def _L0_xattn_ref(q, latent_kv, Wq, Wkv_expand, Wout):
        import jax, jax.numpy as jnp
        import numpy as np
        B, S, H, NH, L = (2, 256, 256, 16, 64)
        HD = H // NH
        b, sq, _ = q.shape
        sk = latent_kv.shape[1]
        qp = q @ Wq.T
        kv = latent_kv @ Wkv_expand.T
        k, v = jnp.split(kv, 2, axis=-1)
        qh = qp.reshape(b, sq, NH, HD).transpose(0, 2, 1, 3)
        kh = k.reshape(b, sk, NH, HD).transpose(0, 2, 1, 3)
        vh = v.reshape(b, sk, NH, HD).transpose(0, 2, 1, 3)
        inv_sqrt_d = 1.0 / jnp.sqrt(jnp.float32(HD))
        scores = jnp.einsum('bhqd,bhkd->bhqk', qh, kh) * inv_sqrt_d
        causal = jnp.tril(jnp.ones((sq, sk), dtype=bool))
        scores = jnp.where(causal, scores, jnp.finfo(scores.dtype).min)
        attn = jax.nn.softmax(scores, axis=-1)
        out = jnp.einsum('bhqk,bhkd->bhqd', attn, vh)
        out = out.transpose(0, 2, 1, 3).reshape(b, sq, H)
        return out @ Wout.T

    def _L0_ffn_ref(hidden_states, gate_w, w_gate, w_up, w_down, sw_gate, sw_up, sw_down):
        import jax, jax.numpy as jnp
        import numpy as np
        NUM_EXPERTS = 8
        TOP_K = 2
        ROUTED_SCALE = 1.0
        D_MODEL = 256
        D_FFN = 176
        B, S, D = hidden_states.shape
        x = hidden_states.reshape(-1, D)
        T = x.shape[0]
        logits = jnp.einsum('td,ed->te', x.astype(jnp.float32), gate_w)
        probs = jax.nn.softmax(logits, axis=-1)
        topk_w, topk_ids = jax.lax.top_k(probs, TOP_K)
        topk_w = topk_w / jnp.sum(topk_w, axis=-1, keepdims=True)
        gates = jnp.zeros((T, NUM_EXPERTS), jnp.float32).at[jnp.arange(T)[:, None], topk_ids].add(topk_w)
        gates = gates.astype(x.dtype)
        g = jnp.einsum('td,edf->etf', x, w_gate)
        u = jnp.einsum('td,edf->etf', x, w_up)
        h = jax.nn.silu(g) * u
        down = jnp.einsum('etf,efd->etd', h, w_down)
        routed = jnp.einsum('te,etd->td', gates, down)
        routed = routed * ROUTED_SCALE
        shared = jax.nn.silu(x @ sw_gate) * (x @ sw_up) @ sw_down
        out = routed + shared
        return out.reshape(B, S, D)
    x = x + _L0_attn_ref(_layernorm(x, axis=-1), L0_attn_Wq, L0_attn_Wk, L0_attn_Wv, L0_attn_Wo)
    x = x + _L0_xattn_ref(_layernorm(x, axis=-1), ctx_512, L0_xattn_Wq, L0_xattn_Wkv_expand, L0_xattn_Wout)
    x = x + _L0_ffn_ref(_layernorm(x, axis=-1), L0_ffn_gate_w, L0_ffn_w_gate, L0_ffn_w_up, L0_ffn_w_down, L0_ffn_sw_gate, L0_ffn_sw_up, L0_ffn_sw_down)
    return x

_drawn_inputs = setup_inputs


def setup_inputs(seed=0):
    import zlib

    import numpy as np

    out = dict(_drawn_inputs(seed))
    spreads = {}
    factors = {'L0_xattn_Wq': 8.0,
     'L0_ffn_gate_w': 6.666,
     'L0_ffn_w_gate': 5.887,
     'L0_ffn_w_up': 5.818,
     'L0_ffn_w_down': 5.818,
     'L0_ffn_sw_gate': 4.195,
     'L0_ffn_sw_up': 4.157,
     'L0_ffn_sw_down': 4.13}
    for name, (base, spread) in spreads.items():
        noise = np.random.default_rng([zlib.crc32(name.encode()), seed]).standard_normal(out[name].shape)
        drawn = base * np.exp(spread * noise) if base else spread * noise
        out[name] = jnp.asarray(drawn.astype(out[name].dtype))
    for name, factor in factors.items():
        out[name] = (out[name] * factor).astype(out[name].dtype)
    return out
```

```python
from contextlib import ExitStack

import concourse.bass as bass
from concourse import mybir

ALU = mybir.AluOpType
ACT = mybir.ActivationFunctionType
F32 = mybir.dt.float32
BF16 = mybir.dt.bfloat16
I32 = mybir.dt.int32
U32 = mybir.dt.uint32
AX = mybir.AxisListType

P = 128
B, S, E = 4, 256, 256
T = B * S
NT = T // P
KC = E // P
H1, G1, D1 = 32, 8, 8
H2, D2, LAT = 16, 16, 64
HG = 4
NX, F = 8, 176
FT = (NX + 1) * F
FC = (FT + P - 1) // P
FCR = NX * F // P
FL = FT - (FC - 1) * P
PARTS = 3
Q_PART = (0, 0, 0, 1, 1, 2)
K_PART = (0, 1, 2, 0, 1, 0)
STACK = len(Q_PART)
EPS = 1e-5
RSQRT_GUESS = 0x5F3759DF
NEWTON = 3
NBANK = 8
MISC = NBANK - 1
VBANK = 6

GROUPS = [(0, b, g) for b in range(B) for g in range(G1)] + [(1, b, g) for b in range(B) for g in range(H2 // HG)]
PER = (G1, H2 // HG)
DH = (D1, D2)
NH = (H1, H2)


class Timeline:

    def __init__(self):
        self.pass1, self.pass2 = {}, {}
        self.items = {}
        self.chain = {}
        ready = {(0, b): 0 for b in range(B)}
        p1 = p2 = -1
        n = 0
        while n < len(GROUPS):
            a, b, _ = GROUPS[n]
            for i in range(PER[a]):
                p1 = max(p1 + 1, ready[a, b])
                self.pass1[p1] = n + i
            self.add(p1 + 1, 1, ("neg", a, b))
            self.chain.setdefault(p1 + 1, []).append(("negmax", a, b))
            p2 = max(p2, p1 + 2)
            for i in range(PER[a]):
                p2 = p2 + 1
                self.pass2[p2] = n + i
                if i % HG == HG - 1:
                    self.hook(p2 + 1, "put", n + i - HG + 1)
            s = p2 + 1
            i = B * a + b + 3
            if i < 2 * B:
                self.hook(p2 + 1, *(("stack_first", i) if i < B else ("stack_k2", i - B)))
            self.hook(s, "store", a, b)
            self.hook(s + 2, "recip", a, b)
            self.hook(s + 4, "scale", a, b)
            self.add(s + 4, 1, ("out", a, b, 0))
            self.add(s + 5, 0, ("out", a, b, 1))
            self.hook(s + 6, "norm_a", a + 1, b)
            self.hook(s + 7, "norm_b", a + 1, b)
            self.add(s + 7, 1, ("turn", a + 1, b, 0))
            self.add(s + 8, 0, ("turn", a + 1, b, 1))
            if a == 0:
                self.add(s + 8, 1, ("q2", b, 0))
                self.add(s + 9, 0, ("q2", b, 1))
                self.hook(s + 9, "split", b, 0)
                self.hook(s + 10, "split", b, 1)
                ready[1, b] = s + 11
            else:
                self.add(s + 8, 1, ("router", b))
                self.hook(s + 9, "gates_a", b)
                self.hook(s + 10, "gates_b", b)
                self.add(s + 10, 1, ("gates", b))
            n += PER[a]
        self.attn_steps = p2 + 2
        self.moe0 = self.attn_steps
        self.steps = self.moe0 + 2 * FC + 1

    def hook(self, s, *what):
        self.chain.setdefault(s, []).append(what)

    def add(self, s, slot, what):
        self.items.setdefault((s, slot), []).append(what)


def rsqrt_steps(eng, link, y, v, t):
    for _ in range(NEWTON):
        link(eng.tensor_tensor(t, y, y, ALU.mult))
        link(eng.tensor_tensor(t, t, v, ALU.mult))
        link(eng.tensor_scalar(t, t, -0.5, 1.5, ALU.mult, ALU.add))
        last = eng.tensor_tensor(y, y, t, ALU.mult)
        if _ < NEWTON - 1:
            link(last)
    return last


def decoder_kernel(nc, x, ctx, wq, wk, wv, wo, xwq, xwkv, xwo, gate_w, w_gate, w_up, w_down, sw_gate, sw_up,
                   sw_down, out):
    line = Timeline()
    with ExitStack() as stack:
        def sb(name, shape, dt=F32):
            return stack.enter_context(nc.sbuf_tensor(name, shape, dt))

        def sem(name):
            return stack.enter_context(nc.semaphore(name))

        def sems(name, n):
            return [sem(f"{name}{i}") for i in range(n)]

        def scratch(name, shape, dt):
            return nc.dram_tensor(name, shape, dt, kind="Internal").ap()

        q_dram = [scratch(f"q_parts{a}", (PARTS, E, T), BF16) for a in range(2)]
        k_dram = [scratch(f"k_parts{a}", (PARTS, G1 * D1 if a == 0 else E, T), BF16) for a in range(2)]
        o_dram = [scratch(f"o_raw{a}", (NH[a], DH[a] + 1, T), F32) for a in range(2)]
        r_dram = [scratch(f"o_scale{a}", (NH[a], T), F32) for a in range(2)]

        ps = stack.enter_context(nc.psum_tensor("ps", [P, NBANK, 512], F32))
        psb = ps[:, :, :].bitcast(BF16)

        res = sb("res", [P, NT, E])
        xn = sb("xn", [P, 2, E])
        xnT = sb("xnT", [P, KC, T])
        stats = sb("stats", [P, 4, 2, 6])
        mean_var = sb("mean_var", [P, 4, 2, 2])
        var_eps = sb("var_eps", [P, 4, 2])
        rstd = sb("rstd", [P, 4, 2])
        newton = sb("newton", [P, 4, 2])
        wo_s = [sb("wo1", [P, KC, E]), sb("wo2", [P, KC, E])]
        wq2 = sb("wq2", [P, KC, E])
        gate_T = sb("gate_T", [P, KC, NX])
        up_g = sb("up_g", [P, KC, FT])
        up_u = sb("up_u", [P, KC, FT])
        down = sb("down", [P, FC, E])
        NQKV = E + 2 * G1 * D1
        shared = sb("shared", [P, KC * NQKV + 3 * KC * E + NX // NX * E + 2 * KC * LAT + 2 * E])
        at = [0]

        def take(n):
            at[0] += n
            return shared[:, at[0] - n:at[0]]

        wqkv = take(KC * NQKV).rearrange("p (c n) -> p c n", c=KC)
        raw = take(KC * E).rearrange("p (c n) -> p c n", c=KC)
        raw2 = take(KC * E).rearrange("p (c n) -> p c n", c=KC)
        raw_kv = take(2 * KC * LAT).rearrange("p (c n) -> p c n", n=LAT)
        raw_gate = take(E)[0:NX, :]
        ctx_s = take(NT * LAT).rearrange("p (t n) -> p t n", t=NT)
        wkv2 = take(2 * E)[0:LAT, :]
        at[0] = 0
        silu = take(2 * 512).rearrange("p (c n) -> p c n", c=2)
        hidden = take(2 * 512).rearrange("p (c n) -> p c n", c=2)
        mid = take(512)
        ident = sb("ident", [P, P])
        identb = sb("identb", [P, P], BF16)
        mask = sb("mask", [P, P], BF16)
        ones = sb("ones", [PARTS, S], BF16)
        select = sb("select", [PARTS * NX, NX * F], BF16)
        number = sb("number", [P, NX])
        NPLACE = 3
        q_stack = sb("q_stack", [STACK * D2 + PARTS, H1, NPLACE, S], BF16)
        k_stack = sb("k_stack", [STACK * D2 + PARTS, H2, NPLACE, S], BF16)
        NPB = 2
        exact = sb("exact", [P, 2 * NPB, S])
        parts = sb("parts", [P, 2 * NPB, PARTS, S], BF16)
        v_s = [sb("v0", [P, NT, G1 * (D1 + 1) + 32]), sb("v1", [P, NT, H2 * (D2 + 1) + 32])]
        v_head = [v_s[a][:, :, 0:(G1, H2)[a] * (DH[a] + 1)].rearrange("p t (h d) -> p t h d", d=DH[a] + 1)
                  for a in range(2)]
        rowmax = sb("rowmax", [P, 2, 2 * H1])
        neg_rest = sb("neg_rest", [P, 2, 2 * H1])
        neg_parts = sb("neg_parts", [P, 2, PARTS, 2 * H1], BF16)
        neg_T = sb("neg_T", [2 * H1, 2, PARTS, P], BF16)
        probs = sb("probs", [P, 2, 3, 512])
        ctx_T = probs[0:LAT, :, :, :].rearrange("p a b c -> p (a b c)")[:, 0:T]
        NRAW = 2 * HG
        o_raw = sb("o_raw", [P, NRAW, S])
        sums = sb("sums", [P, 2, 64])
        o_T = sb("o_T", [P, KC, S])
        r_T = sb("r_T", [P, KC, S])
        o_tok = sb("o_tok", [P, 2, E])
        logits = sb("logits", [P, 2, NX])
        shifted = sb("shifted", [P, 2, NX])
        expd = sb("expd", [P, 2, NX])
        prob = sb("prob", [P, 2, NX])
        small = sb("small", [P, 4, 2])
        top = sb("top", [P, 2, 8])
        top_at = sb("top_at", [P, 2, 8], U32)
        top_w = sb("top_w", [P, 2, 2])
        top_f = sb("top_f", [P, 2, 2])
        gate0 = sb("gate0", [P, 2, NX])
        gate1 = sb("gate1", [P, 2, NX])
        gate_parts = sb("gate_parts", [P, 2, PARTS, NX], BF16)
        gates_T = sb("gates_T", [PARTS * NX, T], BF16)
        s_x = sems("x_loaded", B)
        s_wqkv = sem("wqkv_loaded")
        s_w2 = sem("small_weights_loaded")
        s_moe = sem("expert_weights_loaded")
        s_ones = sem("ones_rows_stored")
        s_sel = sem("select_copied")
        s_const = sem("constants_made")
        s_guess = sem("rstd_guessed")
        s_rstd = sem("rstd_done")
        s_xn = sem("xn_done")
        s_mm = sem("item_in_psum")
        s_item = sem("item_copied_out")
        s_split = [sem("split_by_vector"), sem("split_by_pool")]
        s_parts_out = sems("parts_stored", 2 * NPB)
        s_qst = [sems("q0_stacked", B), sems("q1_stacked", B)]
        s_kst = [sems("k0_stacked", B), sems("k1_stacked", B)]
        s_p1 = sem("scores_for_max")
        s_max = sem("maxima_done")
        s_neg = sem("negmax_parts")
        s_nst = [sems("neg0_stacked", B), sems("neg1_stacked", B)]
        s_p2 = sem("scores_for_exp")
        s_exp = sem("exp_done")
        s_keep = sem("masked")
        s_pv = sem("pv_done")
        s_raw = sem("o_raw_copied")
        s_put = sems("o_raw_stored", len(GROUPS) // HG)
        s_vones = sem("v_ones_set")
        s_sums = sem("sums_loaded")
        s_oT = sem("oT_loaded")
        s_rec = sem("recip_done")
        s_rst = sem("recip_stored")
        s_rT = sem("rT_loaded")
        s_scaled = sem("oT_scaled")
        s_ga = sem("logits_shifted")
        s_gexp = sem("router_exp")
        s_gp = sem("gate_parts_done")
        s_g = sem("gate_proj")
        s_u = sem("up_proj")
        s_e = sem("gates_spread")
        s_silu = sem("silu_done")
        s_h = sem("hidden_done")
        s_down = sem("down_done")
        s_y = sem("result_done")
        s_out = sem("result_stored")
        seq_v = sem("vector_sequence")
        seq_p = sem("pool_sequence")

        def linker(eng, s):
            count = [0]

            def link(ins, n=1):
                count[0] += n
                ins.then_inc(s, n)
                eng.wait_ge(s, count[0])
                return ins

            return link

        first = []
        for b in range(B):
            first += [("turn", 0, b, 0), ("turn", 0, b, 1), ("q1", b, 0), ("q1", b, 1), ("k1", b), ("v1", b)]
        first += [("wT", i) for i in range(6)] + [("ctxT", i) for i in range(2)]
        first += [("k2", b, c) for b in range(B) for c in range(KC)] + [("v2", t) for t in range(NT)]
        later = []
        for s in range(line.steps):
            later += line.items.get((s, 0), []) + line.items.get((s, 1), [])
        number_of = {it: k for k, it in enumerate(first + later)}
        v_pieces = [p for b in range(B) for p in (("q1", b, 0), ("q1", b, 1), ("k1", b))]
        p_pieces = [("k2", b, c) for b in range(B) for c in range(KC)]
        p_pieces += [("q2",) + w[1:] for s in range(line.steps) for w in line.chain.get(s, []) if w[0] == "split"]
        piece_of = {p: (0, i) for i, p in enumerate(v_pieces)} | {p: (1, i) for i, p in enumerate(p_pieces)}

        def buffer_of(piece):
            who, i = piece_of[piece]
            return who * NPB + i % NPB

        def chains(kind):
            found = [w[1:] for s in range(line.steps) for w in line.chain.get(s, []) if w[0] == kind]
            return {w: i for i, w in enumerate(found)}

        order = {k: chains(k) for k in ("negmax", "store", "recip", "scale", "gates_a", "gates_b")}
        norm_of = {(0, b): b for b in range(B)} | {w: B + i for w, i in chains("norm_a").items()}
        NORM_ORDER = {k: ab for ab, k in norm_of.items()}
        last_group = {GROUPS[n][:2]: n for n in range(len(GROUPS))}

        def head_slots(n):
            a, _, g = GROUPS[n]
            return slice(g, H1, G1) if a == 0 else slice(HG * g, HG * g + HG)

        def place_of(a, b):
            return (B * a + b) % NPLACE

        block = stack.enter_context(nc.Block())

        @block.sync
        def _(sp):
            sp.dma_start(res[:, 0:2, :], x[0].rearrange("(h p) e -> p h e", p=P)).then_inc(s_x[0], 16)
            for w, at, n in ((wq, 0, E), (wk, E, G1 * D1), (wv, E + G1 * D1, G1 * D1)):
                sp.dma_start(wqkv[:, :, at:at + n], w.rearrange("(c p) n -> p c n", p=P)).then_inc(s_wqkv, 16)
            for b in range(1, B):
                sp.dma_start(res[:, 2 * b:2 * b + 2, :], x[b].rearrange("(h p) e -> p h e", p=P)).then_inc(s_x[b], 16)
            small_w = ((raw, xwq), (raw2, xwo), (raw_kv, xwkv), (wo_s[0], wo))
            for dst, src in small_w:
                sp.dma_start(dst[:, :, :], src.rearrange("(c p) n -> p c n", p=P)).then_inc(s_w2, 16)
            sp.dma_start(raw_gate[:, :], gate_w).then_inc(s_w2, 16)
            sp.dma_start(ctx_s[:, :, :], ctx.rearrange("b (h p) l -> p (b h) l", p=P)).then_inc(s_w2, 16)
            sp.wait_ge(s_const, 1)
            r = STACK * D2
            for place in range(NPLACE):
                sp.dma_start(k_stack[r:r + PARTS, :, place, :],
                             ones[:, None, :].to_broadcast([PARTS, H2, S])).then_inc(s_ones, 16)
            for p in range(1, PARTS):
                sp.dma_start(select[NX * p:NX * p + NX, :], select[0:NX, :]).then_inc(s_sel, 16)

            def store_parts(piece):
                kind, b, *c = piece
                who, i = piece_of[piece]
                a = 0 if kind in ("q1", "k1") else 1
                dram = (q_dram if kind[0] == "q" else k_dram)[a]
                rows = min(P, dram.shape[1])
                r = P * c[0] if c else 0
                buf = buffer_of(piece)
                sp.wait_ge(s_split[who], i + 1)
                sp.dma_start(dram[:, r:r + rows, b * S:b * S + S].rearrange("j r t -> r j t"),
                             parts[0:rows, buf, :, :]).then_inc(s_parts_out[buf], 16)

            def stored(piece):
                sp.wait_ge(s_parts_out[buffer_of(piece)], 16 * (piece_of[piece][1] // NPB + 1))

            def load_stack(dst, dram, a, order_of_parts, b, s):
                d = DH[a]
                place = place_of(a, b)
                for j, part in enumerate(order_of_parts):
                    sp.dma_start(dst[d * j:d * j + d, 0:dram.shape[1] // d, place, :],
                                 dram[part, :, b * S:b * S + S].rearrange("(h d) t -> d h t", d=d)).then_inc(s, 16)

            def place_free(a, b):
                i = B * a + b - NPLACE
                if i >= 0:
                    sp.wait_ge(s_p2, 2 * last_group[i // B, i % B] + 2)

            def store_first(b):
                for p in (("q1", b, 0), ("q1", b, 1), ("k1", b)):
                    store_parts(p)

            def stack_first(b):
                for p in (("q1", b, 0), ("q1", b, 1), ("k1", b)):
                    stored(p)
                place_free(0, b)
                load_stack(q_stack, q_dram[0], 0, Q_PART, b, s_qst[0][b])
                load_stack(k_stack, k_dram[0], 0, K_PART, b, s_kst[0][b])
                r = STACK * D1
                sp.dma_start(k_stack[r:r + PARTS, 0:G1, place_of(0, b), :],
                             ones[:, None, :].to_broadcast([PARTS, G1, S])).then_inc(s_kst[0][b], 16)

            for b in range(B):
                store_first(b)
                if b < NPLACE:
                    stack_first(b)
            for b in range(B):
                for c in range(KC):
                    store_parts(("k2", b, c))
            for kc in range(KC):
                for dst, many, one in ((up_g, w_gate, sw_gate), (up_u, w_up, sw_up)):
                    sp.dma_start(dst[:, kc, 0:NX * F].rearrange("p (e f) -> p e f", e=NX),
                                 many[:, P * kc:P * kc + P, :].rearrange("e p f -> p e f")).then_inc(s_moe, 16)
                    sp.dma_start(dst[:, kc, NX * F:FT], one[P * kc:P * kc + P, :]).then_inc(s_moe, 16)
            sp.dma_start(down[:, 0:FCR, :], w_down.rearrange("e f n -> (e f) n").rearrange("(c p) n -> p c n", p=P))\
              .then_inc(s_moe, 16)
            sp.dma_start(down[:, FCR, :], sw_down[0:P, :]).then_inc(s_moe, 16)
            sp.dma_start(down[0:FL, FC - 1, :], sw_down[P:F, :]).then_inc(s_moe, 16)

            for s in range(line.steps):
                for what, *arg in line.chain.get(s, []):
                    if what == "stack_first":
                        stack_first(*arg)
                    if what == "stack_k2":
                        b, = arg
                        for c in range(KC):
                            stored(("k2", b, c))
                        place_free(1, b)
                        load_stack(k_stack, k_dram[1], 1, K_PART, b, s_kst[1][b])
                    if what == "put":
                        n0, = arg
                        a, b, g0 = GROUPS[n0]
                        d = DH[a]
                        tok = slice(b * S, b * S + S)
                        sp.wait_ge(s_raw, n0 + HG)
                        for j in range(HG):
                            hs = slice(G1 * j + g0, G1 * j + g0 + HG) if a == 0 else slice(j, H2, HG)
                            sp.dma_start(o_dram[a][hs, :, tok].rearrange("h d t -> d h t"),
                                         o_raw[32 * j:32 * j + d + 1, n0 % NRAW:n0 % NRAW + HG, :])\
                              .then_inc(s_put[n0 // HG], 16)
                    if what == "negmax":
                        a, b = arg
                        i = order["negmax"][a, b]
                        r = STACK * DH[a]
                        sp.wait_ge(s_item, number_of["neg", a, b] + 1)
                        for p in range(PARTS):
                            for qb in range(2):
                                sp.dma_start(q_stack[r + p:r + p + 1, 0:NH[a], place_of(a, b), qb * P:qb * P + P],
                                             neg_T[qb * NH[a]:(qb + 1) * NH[a], i % 2, p, :])\
                                  .then_inc(s_nst[a][b], 16)
                    if what == "store":
                        a, b = arg
                        i = order["store"][a, b]
                        d = DH[a]
                        tok = slice(b * S, b * S + S)
                        for n0 in range(last_group[a, b] + 1 - PER[a], last_group[a, b], HG):
                            sp.wait_ge(s_put[n0 // HG], 16 * HG)
                        w = NH[a] * S // P
                        if i >= 1:
                            sp.wait_ge(s_scaled, i)
                            sp.wait_ge(s_mm, number_of["out", (i - 1) // B, (i - 1) % B, 1] + 1)
                        sp.dma_start(sums[:, i % 2, 0:w],
                                     o_dram[a][:, d, tok].rearrange("h (c w) -> h c w", w=w)).then_inc(s_sums, 16)
                        for c in range(KC):
                            hc = P // d
                            sp.dma_start(o_T[:, c, :], o_dram[a][hc * c:hc * c + hc, 0:d, tok]).then_inc(s_oT, 16)
                        sp.wait_ge(s_rec, i + 1)
                        sp.dma_start(r_dram[a][:, tok].rearrange("h (c w) -> h c w", w=w),
                                     sums[:, i % 2, 0:w]).then_inc(s_rst, 16)
                        sp.wait_ge(s_rst, 16 * (i + 1))
                        for c in range(KC):
                            sp.dma_start(r_T[:, c, :],
                                         r_dram[a][hc * c:hc * c + hc, None, tok].to_broadcast([hc, d, S]))\
                              .then_inc(s_rT, 16)
                    if what == "split":
                        b, c = arg
                        store_parts(("q2", b, c))
                        if c == KC - 1:
                            for k in range(KC):
                                stored(("q2", b, k))
                            place_free(1, b)
                            load_stack(q_stack, q_dram[1], 1, Q_PART, b, s_qst[1][b])
                if s in (line.moe0 + FC, line.moe0 + 2 * FC):
                    hf = 0 if s == line.moe0 + FC else 1
                    for k in range(2):
                        sp.wait_ge(s_y, 2 * hf + k + 1)
                        sp.dma_start(out[2 * hf + k].rearrange("(h p) e -> p h e", p=P),
                                     res[:, 4 * hf + 2 * k:4 * hf + 2 * k + 2, :]).then_inc(s_out, 16)
            sp.wait_ge(s_out, 16 * B)

        def split_parts(eng, link, buf, rows):
            hi, mid_, lo = (parts[0:rows, buf, j, :] for j in range(PARTS))
            r = exact[0:rows, buf, :]
            link(eng.tensor_tensor(r, r, hi, ALU.subtract))
            link(eng.tensor_copy(mid_, r))
            return eng.tensor_tensor(lo, r, mid_, ALU.subtract)

        @block.gpsimd
        def _(pool):
            link = linker(pool, seq_p)
            pool.memset(v_s[0][:, :, :], 1.0).then_inc(s_vones, 1)
            pool.memset(v_s[1][:, :, :], 1.0).then_inc(s_vones, 1)
            pool.memset(ones[:, :], 1.0)
            pool.memset(mask[:, :], 0.0)
            pool.memset(select[0:NX, :], 1.0)
            for e in range(NX):
                pool.memset(number[:, e:e + 1], float(e))
            link(pool.memset(ident[:, :], 0.0))
            link(pool.affine_select(out=ident[:, :], in_=ident[:, :], compare_op=ALU.not_equal, fill=1.0, base=0,
                                    pattern=[[-1, P]], channel_multiplier=1))
            pool.tensor_copy(identb[:, :], ident[:, :])
            pool.affine_select(out=mask[:, :], in_=mask[:, :], compare_op=ALU.is_ge, fill=-1e30, base=0,
                               pattern=[[-1, P]], channel_multiplier=1)
            link(pool.affine_select(out=select[0:NX, :], in_=select[0:NX, :], compare_op=ALU.is_ge, fill=0.0,
                                    base=0, pattern=[[1, NX * F]], channel_multiplier=-F))
            pool.affine_select(out=select[0:NX, :], in_=select[0:NX, :], compare_op=ALU.is_ge, fill=0.0,
                               base=F - 1, pattern=[[-1, NX * F]], channel_multiplier=F).then_inc(s_const, 1)

            def rsqrt(k):
                pool.wait_ge(s_guess, k + 1)
                rsqrt_steps(pool, link, rstd[:, k % 4, :], var_eps[:, k % 4, :], newton[:, k % 4, :])\
                    .then_inc(s_rstd, 1)

            def split(piece):
                _, i = piece_of[piece]
                buf = buffer_of(piece)
                pool.wait_ge(s_item, number_of[piece] + 1)
                split_parts(pool, link, buf, P).then_inc(s_split[1], 1)

            for b in range(B):
                rsqrt(b)
            for b in range(B):
                for c in range(KC):
                    split(("k2", b, c))
            for s in range(line.steps):
                if s in line.pass2:
                    n = line.pass2[s]
                    for u, count in ((0, 2 * n + 1), (2, 2 * n + 2)):
                        blk = probs[:, n % 2, u, :].rearrange("p (h q) -> p h q", h=HG)
                        pool.wait_ge(s_exp, count)
                        pool.affine_select(out=blk, in_=blk, compare_op=ALU.is_ge, fill=0.0, base=0,
                                           pattern=[[0, HG], [1, P]], channel_multiplier=-1).then_inc(s_keep, 1)
                for what, *arg in line.chain.get(s, []):
                    if what == "norm_a":
                        rsqrt(norm_of[tuple(arg)])
                    if what == "split":
                        split(("q2", *arg))

        @block.scalar
        def _(act):
            def copy(dst, src, scale=None):
                return act.activation(dst, src, ACT.Copy, scale=scale) if scale else act.copy(dst, src)

            def copy_item(it):
                k = number_of[it]
                bank = k % NBANK if k < len(first) else MISC
                act.wait_ge(s_mm, k + 1)
                kind = it[0]
                if kind == "turn":
                    t = 2 * it[2] + it[3]
                    last = copy(xnT[:, :, P * t:P * t + P], ps[:, bank, 0:KC * P].rearrange("p (c t) -> p c t", c=KC))
                elif kind in ("q1", "q2", "k1", "k2"):
                    piece = it
                    who, i = piece_of[piece]
                    buf = buffer_of(piece)
                    rows = G1 * D1 if kind == "k1" else P
                    scale = {"q1": D1 ** -0.5, "q2": D2 ** -0.5}.get(kind)
                    if i >= NPB:
                        act.wait_ge(s_split[who], i - NPB + 1)
                        act.wait_ge(s_parts_out[buf], 16 * (i // NPB))
                    copy(exact[0:rows, buf, :], ps[0:rows, bank, 0:S], scale)
                    last = copy(parts[0:rows, buf, 0, :], ps[0:rows, bank, 0:S], scale)
                elif kind == "v1":
                    b = it[1]
                    act.wait_ge(s_vones, 1)
                    last = copy(v_head[0][:, 2 * b:2 * b + 2, :, 0:D1],
                                ps[:, bank, 0:2 * G1 * D1].rearrange("p (t g d) -> p t g d", t=2, d=D1))
                elif kind == "v2":
                    act.wait_ge(s_vones, 2)
                    last = copy(v_head[1][:, it[1], :, 0:D2], ps[:, bank, 0:E].rearrange("p (h d) -> p h d", d=D2))
                elif kind == "wT":
                    i = it[1]
                    if i < 4:
                        last = copy((wq2, wo_s[1])[i // 2][:, i % 2, :], ps[:, bank, 0:E])
                    elif i == 4:
                        last = copy(wkv2[:, :], ps[0:LAT, bank, :])
                    else:
                        last = copy(gate_T[:, :, :], ps[:, bank, 0:KC * NX].rearrange("p (c e) -> p c e", c=KC))
                elif kind == "ctxT":
                    last = copy(ctx_T[:, 512 * it[1]:512 * it[1] + 512], ps[0:LAT, bank, :])
                elif kind == "neg":
                    a, b = it[1:]
                    i = order["negmax"][a, b]
                    if i >= 2:
                        a0, b0 = (i - 2) // B, (i - 2) % B
                        act.wait_ge(s_nst[a0][b0], 16 * 2 * PARTS)
                    last = copy(neg_T[0:2 * NH[a], i % 2, :, :],
                                psb[0:2 * NH[a], bank, 0:PARTS * P].rearrange("p (j t) -> p j t", j=PARTS))
                elif kind == "out":
                    last = copy(o_tok[:, it[3], :], ps[:, bank, 0:E])
                elif kind == "router":
                    last = copy(logits[:, :, :], ps[:, bank, 0:2 * NX].rearrange("p (t e) -> p t e", t=2))
                else:
                    b = it[1]
                    last = copy(gates_T[:, b * S:b * S + S], psb[0:PARTS * NX, bank, 0:S])
                last.then_inc(s_item, 1)

            for it in first:
                copy_item(it)
            for s in range(line.steps):
                for it in line.items.get((s, 0), []):
                    copy_item(it)
                n = line.pass2.get(s)
                if n is not None:
                    act.wait_ge(s_p2, 2 * n + 1)
                    if n >= 2:
                        act.wait_ge(s_pv, n - 1)
                    act.activation(probs[:, n % 2, 0, :], ps[:, 3, :], ACT.Exp).then_inc(s_exp, 1)
                before = line.pass2.get(s - 1)
                if before is not None:
                    act.wait_ge(s_pv, before + 1)
                    if before >= NRAW:
                        act.wait_ge(s_put[(before - NRAW) // HG], 16 * HG)
                    copy(o_raw[:, before % NRAW, :], ps[:, VBANK, 0:S]).then_inc(s_raw, 1)
                for it in line.items.get((s, 1), []):
                    copy_item(it)
                if n is not None:
                    act.wait_ge(s_p2, 2 * n + 2)
                    act.activation(probs[:, n % 2, 1:3, :], ps[:, 4:6, :], ACT.Exp).then_inc(s_exp, 1)
                c = s - line.moe0
                if 0 <= c < 2 * FC:
                    rows = FL if c % FC == FC - 1 else P
                    act.wait_ge(s_g, c + 1)
                    if c >= 2:
                        act.wait_ge(s_h, c - 1)
                    act.activation(silu[0:rows, c % 2, :], ps[0:rows, c % 2, :], ACT.Silu).then_inc(s_silu, 1)
                for what, *arg in line.chain.get(s, []):
                    if what == "gates_a":
                        act.wait_ge(s_ga, order["gates_a"][tuple(arg)] + 1)
                        act.activation(expd[:, :, :], shifted[:, :, :], ACT.Exp).then_inc(s_gexp, 1)

        @block.vector
        def _(dve):
            link = linker(dve, seq_v)

            def norm_a(a, b):
                k = norm_of[a, b]
                r = k % 4
                for h in range(2):
                    last = dve.bn_stats(stats[:, r, h, :], res[:, 2 * b + h, :])
                    link(last)
                for h in range(2):
                    link(dve.bn_aggr(mean_var[:, r, h, :], stats[:, r, h, :]))
                link(dve.tensor_scalar(var_eps[:, r, :], mean_var[:, r, :, 1], EPS, None, ALU.add))
                link(dve.tensor_scalar(rstd[:, r, :].bitcast(I32), var_eps[:, r, :].bitcast(I32), 1, None,
                                       ALU.arith_shift_right))
                dve.tensor_scalar(rstd[:, r, :].bitcast(I32), rstd[:, r, :].bitcast(I32), -1, RSQRT_GUESS,
                                  ALU.mult, ALU.add).then_inc(s_guess, 1)

            def norm_b(a, b):
                k = norm_of[a, b]
                r = k % 4
                dve.wait_ge(s_rstd, k + 1)
                if k >= 1:
                    a0, b0 = NORM_ORDER[k - 1]
                    dve.wait_ge(s_mm, number_of["turn", a0, b0, 1] + 1)
                for h in range(2):
                    dve.tensor_scalar(xn[:, h, :], res[:, 2 * b + h, :], mean_var[:, r, h, 0:1],
                                      rstd[:, r, h:h + 1], ALU.subtract, ALU.mult).then_inc(s_xn, 1)

            def split(piece):
                who, i = piece_of[piece]
                buf = buffer_of(piece)
                dve.wait_ge(s_item, number_of[piece] + 1)
                rows = G1 * D1 if piece[0] == "k1" else P
                split_parts(dve, link, buf, rows).then_inc(s_split[0], 1)

            def gates(b):
                i = order["gates_b"][b,]
                total, inv, den, rden = (small[:, k, :] for k in range(4))
                dve.wait_ge(s_gexp, i + 1)
                link(dve.tensor_reduce(total, expd[:, :, :], AX.X, ALU.add))
                link(dve.reciprocal(inv, total))
                link(dve.tensor_tensor(prob[:, :, :], expd[:, :, :], inv[:, :, None].to_broadcast([P, 2, NX]),
                                       ALU.mult))
                for h in range(2):
                    link(dve.max(top[:, h, :], prob[:, h, :]))
                for h in range(2):
                    link(dve.max_index(top_at[:, h, :], top[:, h, :], prob[:, h, :]))
                link(dve.tensor_copy(top_f[:, :, :], top_at[:, :, 0:2]))
                link(dve.tensor_tensor(den, top[:, :, 0], top[:, :, 1], ALU.add))
                link(dve.reciprocal(rden, den))
                link(dve.tensor_tensor(top_w[:, :, :], top[:, :, 0:2], rden[:, :, None].to_broadcast([P, 2, 2]),
                                       ALU.mult))
                for h in range(2):
                    for k, gate in enumerate((gate0, gate1)):
                        link(dve.tensor_scalar(gate[:, h, :], number[:, :], top_f[:, h, k:k + 1],
                                               top_w[:, h, k:k + 1], ALU.is_equal, ALU.mult))
                link(dve.tensor_tensor(gate0[:, :, :], gate0[:, :, :], gate1[:, :, :], ALU.add))
                hi, mi, lo = (gate_parts[:, :, j, :] for j in range(PARTS))
                link(dve.tensor_copy(hi, gate0[:, :, :]))
                link(dve.tensor_tensor(gate1[:, :, :], gate0[:, :, :], hi, ALU.subtract))
                link(dve.tensor_copy(mi, gate1[:, :, :]))
                dve.tensor_tensor(lo, gate1[:, :, :], mi, ALU.subtract).then_inc(s_gp, 1)

            for b in range(B + 1):
                if b < B:
                    dve.wait_ge(s_x[b], 16)
                    norm_a(0, b)
                    norm_b(0, b)
                if b >= 1:
                    for p in (("q1", b - 1, 0), ("q1", b - 1, 1), ("k1", b - 1)):
                        split(p)

            for s in range(line.steps):
                for what, *arg in line.chain.get(s, []):
                    if what == "negmax":
                        a, b = arg
                        i = order["negmax"][a, b]
                        w = 2 * NH[a]
                        m, r = rowmax[:, i % 2, 0:w], neg_rest[:, i % 2, 0:w]
                        hi, mi, lo = (neg_parts[:, i % 2, j, 0:w] for j in range(PARTS))
                        dve.wait_ge(s_max, 2 * last_group[a, b] + 2)
                        link(dve.tensor_scalar(m, m, -1.0, None, ALU.mult))
                        link(dve.tensor_copy(hi, m))
                        link(dve.tensor_tensor(r, m, hi, ALU.subtract))
                        link(dve.tensor_copy(mi, r))
                        dve.tensor_tensor(lo, r, mi, ALU.subtract).then_inc(s_neg, 1)
                    if what == "recip":
                        a, b = arg
                        i = order["recip"][a, b]
                        w = NH[a] * S // P
                        dve.wait_ge(s_sums, 16 * (i + 1))
                        dve.reciprocal(sums[:, i % 2, 0:w], sums[:, i % 2, 0:w]).then_inc(s_rec, 1)
                    if what == "scale":
                        a, b = arg
                        i = order["scale"][a, b]
                        dve.wait_ge(s_oT, 16 * KC * (i + 1))
                        dve.wait_ge(s_rT, 16 * KC * (i + 1))
                        dve.tensor_tensor(o_T[:, :, :], o_T[:, :, :], r_T[:, :, :], ALU.mult).then_inc(s_scaled, 1)
                    if what == "norm_a":
                        a, b = arg
                        dve.wait_ge(s_item, number_of["out", a - 1, b, 1] + 1)
                        link(dve.tensor_tensor(res[:, 2 * b:2 * b + 2, :], res[:, 2 * b:2 * b + 2, :],
                                               o_tok[:, :, :], ALU.add))
                        norm_a(a, b)
                    if what == "norm_b":
                        norm_b(*arg)
                    if what == "gates_a":
                        b, = arg
                        dve.wait_ge(s_item, number_of["router", b] + 1)
                        link(dve.tensor_reduce(small[:, 0, :], logits[:, :, :], AX.X, ALU.max))
                        dve.tensor_tensor(shifted[:, :, :], logits[:, :, :],
                                          small[:, 0, :, None].to_broadcast([P, 2, NX]), ALU.subtract)\
                            .then_inc(s_ga, 1)
                    if what == "gates_b":
                        gates(*arg)
                n = line.pass1.get(s)
                if n is not None:
                    a, b, g = GROUPS[n]
                    i = order["negmax"][a, b]
                    m = rowmax[:, i % 2, :]
                    hs = head_slots(n)
                    dve.wait_ge(s_p1, 2 * n + 1)
                    dve.tensor_reduce(m[:, 0:NH[a]][:, hs], ps[:, 0, :].rearrange("p (h k) -> p h k", h=HG),
                                      AX.X, ALU.max).then_inc(s_max, 1)
                    dve.wait_ge(s_p1, 2 * n + 2)
                    dve.tensor_reduce(m[:, NH[a]:2 * NH[a]][:, hs],
                                      ps[:, 1:3, :].rearrange("p u (h k) -> p h u k", h=HG),
                                      AX.XY, ALU.max).then_inc(s_max, 1)
                c = s - line.moe0
                if 0 <= c < 2 * FC:
                    fc = c % FC
                    rows = FL if fc == FC - 1 else P
                    dve.wait_ge(s_silu, c + 1)
                    dve.wait_ge(s_u, c + 1)
                    if c >= 2:
                        dve.wait_ge(s_down, c - 1)
                    if c >= 1:
                        dve.wait_ge(s_h, c)
                    if fc < FCR:
                        link(dve.tensor_tensor(mid[:, :], silu[:, c % 2, :], ps[:, 2 + c % 2, :], ALU.mult))
                        dve.wait_ge(s_e, FCR * (c // FC) + fc + 1)
                        dve.tensor_tensor(hidden[:, c % 2, :], mid[:, :], ps[:, 4, :], ALU.mult).then_inc(s_h, 1)
                    else:
                        dve.tensor_tensor(hidden[0:rows, c % 2, :], silu[0:rows, c % 2, :],
                                          ps[0:rows, 2 + c % 2, :], ALU.mult).then_inc(s_h, 1)
                if c in (FC, 2 * FC):
                    hf = c // FC - 1
                    dve.wait_ge(s_down, FC * (hf + 1))
                    for k in range(2):
                        tiles = res[:, 4 * hf + 2 * k:4 * hf + 2 * k + 2, :]
                        dve.tensor_tensor(tiles, ps[:, 5 + k, :].rearrange("p (t e) -> p t e", t=2), tiles,
                                          ALU.add).then_inc(s_y, 1)

        @block.tensor
        def _(pe):
            def mm(dst, lhsT, rhs, start=True, stop=True):
                return pe.matmul(dst, lhsT, rhs, start=start, stop=stop)

            def item(it):
                k = number_of[it]
                bank = k % NBANK if k < len(first) else MISC
                if k >= len(first):
                    pe.wait_ge(s_item, k)
                elif k >= NBANK:
                    pe.wait_ge(s_item, k - NBANK + 1)
                kind = it[0]
                dst = ps[:, bank, :]
                if kind == "turn":
                    _, a, b, h = it
                    pe.wait_ge(s_xn, 2 * norm_of[a, b] + h + 1)
                    for c in range(KC):
                        last = pe.transpose(dst[:, P * c:P * c + P], xn[:, h, P * c:P * c + P], ident[:, :])
                elif kind in ("q1", "q2", "k1"):
                    b = it[1]
                    pe.wait_ge(s_item, number_of["turn", 1 if kind == "q2" else 0, b, 1] + 1)
                    m = G1 * D1 if kind == "k1" else P
                    w, c0 = (wq2, P * it[2]) if kind == "q2" else (wqkv, E if kind == "k1" else P * it[2])
                    for c in range(KC):
                        last = mm(dst[0:m, 0:S], w[:, c, c0:c0 + m], xnT[:, c, b * S:b * S + S], c == 0, c == KC - 1)
                elif kind == "v1":
                    b = it[1]
                    w = G1 * D1
                    for h in range(2):
                        t = 2 * b + h
                        for c in range(KC):
                            last = mm(dst[:, w * h:w * h + w], xnT[:, c, P * t:P * t + P],
                                      wqkv[:, c, E + w:E + 2 * w], c == 0, c == KC - 1)
                elif kind == "wT":
                    i = it[1]
                    if i < 4:
                        src = (raw, raw2)[i // 2]
                        for c in range(KC):
                            last = pe.transpose(dst[:, P * c:P * c + P], src[:, c, P * (i % 2):P * (i % 2) + P],
                                                ident[:, :])
                    elif i == 4:
                        for c in range(2 * KC):
                            last = pe.transpose(dst[0:LAT, P * c:P * c + P], raw_kv[:, c, :], ident[:, :])
                    else:
                        for c in range(KC):
                            last = pe.transpose(dst[:, NX * c:NX * c + NX], raw_gate[:, P * c:P * c + P],
                                                ident[0:NX, 0:NX])
                elif kind == "ctxT":
                    for t in range(4):
                        last = pe.transpose(dst[0:LAT, P * t:P * t + P], ctx_s[:, 4 * it[1] + t, :], ident[:, :])
                elif kind == "k2":
                    _, b, c = it
                    pe.wait_ge(s_item, number_of["ctxT", 1] + 1)
                    last = mm(dst[:, 0:S], wkv2[:, P * c:P * c + P], ctx_T[:, b * S:b * S + S])
                elif kind == "v2":
                    t = it[1]
                    last = mm(dst[:, 0:E], ctx_T[:, P * t:P * t + P], wkv2[:, E:2 * E])
                elif kind == "neg":
                    _, a, b = it
                    i = order["negmax"][a, b]
                    w = 2 * NH[a]
                    pe.wait_ge(s_neg, i + 1)
                    for j in range(PARTS):
                        last = pe.transpose(psb[0:w, bank, P * j:P * j + P], neg_parts[:, i % 2, j, 0:w],
                                            identb[:, :])
                elif kind == "out":
                    _, a, b, h = it
                    pe.wait_ge(s_scaled, order["scale"][a, b] + 1)
                    for c in range(KC):
                        last = mm(dst[:, 0:E], o_T[:, c, P * h:P * h + P], wo_s[a][:, c, :], c == 0, c == KC - 1)
                elif kind == "router":
                    b = it[1]
                    pe.wait_ge(s_item, number_of["turn", 2, b, 1] + 1)
                    for h in range(2):
                        t = 2 * b + h
                        for c in range(KC):
                            last = mm(dst[:, NX * h:NX * h + NX], xnT[:, c, P * t:P * t + P], gate_T[:, c, :],
                                      c == 0, c == KC - 1)
                else:
                    b = it[1]
                    pe.wait_ge(s_gp, order["gates_b"][b,] + 1)
                    for h in range(2):
                        last = pe.transpose(psb[0:PARTS * NX, bank, P * h:P * h + P],
                                            gate_parts[:, h, :, :].rearrange("p j e -> p (j e)"), identb[:, :])
                last.then_inc(s_mm, 1)

            def scores_max(n, blocks):
                a, b, g = GROUPS[n]
                rows = STACK * DH[a]
                place = place_of(a, b)
                heads = range(H1)[head_slots(n)]
                for bank, qb, kb in blocks:
                    if qb == kb:
                        mm(ps[:, bank, :], identb[:, :], mask[:, None, :].to_broadcast([P, HG, P]), True, False)
                    for j, h in enumerate(heads):
                        last = mm(ps[:, bank, P * j:P * j + P],
                                  q_stack[0:rows, h, place, P * qb:P * qb + P],
                                  k_stack[0:rows, g if a == 0 else h, place, P * kb:P * kb + P],
                                  qb != kb, qb != kb or j == HG - 1)
                last.then_inc(s_p1, 1)

            def scores_exp(n, blocks):
                a, b, g = GROUPS[n]
                rows = STACK * DH[a] + PARTS
                place = place_of(a, b)
                for bank, qb, kb in blocks:
                    q = q_stack[0:rows, head_slots(n), place, P * qb:P * qb + P]
                    if a == 0:
                        last = mm(ps[:, bank, :], k_stack[0:rows, g, place, P * kb:P * kb + P], q)
                        continue
                    for j, h in enumerate(range(H1)[head_slots(n)]):
                        last = mm(ps[:, bank, P * j:P * j + P], k_stack[0:rows, h, place, P * kb:P * kb + P],
                                  q_stack[0:rows, h, place, P * qb:P * qb + P])
                last.then_inc(s_p2, 1)

            def weigh(n):
                a, b, g = GROUPS[n]
                d = DH[a] + 1
                pe.wait_ge(s_keep, 2 * n + 2)
                if n >= 1:
                    pe.wait_ge(s_raw, n)
                heads = [g if a == 0 else h for h in range(H1)[head_slots(n)]]
                for kb in range(2):
                    for j, h in enumerate(heads):
                        last = mm(ps[32 * j:32 * j + 32, VBANK, P * kb:S],
                                  v_s[a][:, 2 * b + kb, d * h:d * h + 32],
                                  probs[:, n % 2, 2 * kb:2, P * j:P * j + P] if kb == 0 else
                                  probs[:, n % 2, 2, P * j:P * j + P], kb == 0, kb == 1)
                last.then_inc(s_pv, 1)

            pe.wait_ge(s_const, 1)
            pe.wait_ge(s_wqkv, 16 * 3)
            for it in first:
                if it == ("wT", 0):
                    pe.wait_ge(s_w2, 16 * 6)
                item(it)
            pe.wait_ge(s_item, len(first))
            pe.wait_ge(s_ones, 16 * NPLACE)
            for s in range(line.steps):
                for it in line.items.get((s, 0), []):
                    item(it)
                m, n, before = line.pass1.get(s), line.pass2.get(s), line.pass2.get(s - 1)
                if m is not None:
                    a, b, g = GROUPS[m]
                    if g == 0:
                        pe.wait_ge(s_qst[a][b], 16 * STACK)
                        pe.wait_ge(s_kst[a][b], 16 * (STACK + 1 - a))
                    if m >= 1:
                        pe.wait_ge(s_max, 2 * m - 1)
                    scores_max(m, [(0, 0, 0)])
                if n is not None:
                    a, b, g = GROUPS[n]
                    if g == 0:
                        pe.wait_ge(s_nst[a][b], 16 * 2 * PARTS)
                    if n >= 1:
                        pe.wait_ge(s_exp, 2 * n - 1)
                    scores_exp(n, [(3, 0, 0)])
                if before is not None:
                    weigh(before)
                for it in line.items.get((s, 1), []):
                    item(it)
                if m is not None:
                    if m >= 1:
                        pe.wait_ge(s_max, 2 * m)
                    scores_max(m, [(1, 1, 0), (2, 1, 1)])
                if n is not None:
                    if n >= 1:
                        pe.wait_ge(s_exp, 2 * n)
                    scores_exp(n, [(4, 1, 0), (5, 1, 1)])
                c = s - line.moe0
                if c == 0:
                    pe.wait_ge(s_raw, len(GROUPS))
                    pe.wait_ge(s_moe, 16 * (4 * KC + 3))
                    pe.wait_ge(s_sel, 16 * (PARTS - 1))
                if 0 <= c < 2 * FC:
                    hf, fc = divmod(c, FC)
                    m = FL if fc == FC - 1 else P
                    if fc == 0:
                        pe.wait_ge(s_item, number_of["gates", 2 * hf + 1] + 1)
                    tok = slice(512 * hf, 512 * hf + 512)
                    if c >= 2:
                        pe.wait_ge(s_h, c - 1)
                    for w, bank, done in ((up_g, 0, s_g), (up_u, 2, s_u)):
                        for k in range(KC):
                            last = mm(ps[0:m, bank + c % 2, :], w[:, k, P * fc:P * fc + m], xnT[:, k, tok],
                                      k == 0, k == KC - 1)
                        last.then_inc(done, 1)
                    if fc < FCR:
                        if c >= 1:
                            pe.wait_ge(s_h, c)
                        mm(ps[:, 4, :], select[:, P * fc:P * fc + P], gates_T[:, tok]).then_inc(s_e, 1)
                if 1 <= c <= 2 * FC:
                    hf, fc = divmod(c - 1, FC)
                    r = FL if fc == FC - 1 else P
                    pe.wait_ge(s_h, c)
                    if fc == 0 and hf == 1:
                        pe.wait_ge(s_y, 2)
                    for t in range(4):
                        last = pe.matmul(ps[:, 5 + t // 2, E * (t % 2):E * (t % 2) + E],
                                         hidden[0:r, (c - 1) % 2, P * t:P * t + P], down[0:r, fc, :],
                                         start=fc == 0 and t % 2 == 0, stop=fc == FC - 1,
                                         skip_group_check=True)
                    last.then_inc(s_down, 1)


_INS = ["x", "ctx_512", "L0_attn_Wq", "L0_attn_Wk", "L0_attn_Wv", "L0_attn_Wo", "L0_xattn_Wq",
        "L0_xattn_Wkv_expand", "L0_xattn_Wout", "L0_ffn_gate_w", "L0_ffn_w_gate", "L0_ffn_w_up", "L0_ffn_w_down",
        "L0_ffn_sw_gate", "L0_ffn_sw_up", "L0_ffn_sw_down"]


def kernel(**inputs):
    import numpy as np
    import concourse.bacc as bacc
    from concourse.bass_utils import run_bass_kernel_spmd

    nc = bacc.Bacc("TRN2", target_bir_lowering=False, num_devices=1)
    arrays, args = {}, []
    for name in _INS:
        a = np.ascontiguousarray(inputs[name])
        arrays[f"in_{name}"] = a
        args.append(nc.dram_tensor(f"in_{name}", a.shape, mybir.dt.from_np(a.dtype), kind="ExternalInput").ap())
    args.append(nc.dram_tensor("out", (B, S, E), F32, kind="ExternalOutput").ap())
    decoder_kernel(nc, *args)
    r = run_bass_kernel_spmd(nc, [arrays], core_ids=[0])
    return r.results[0]["out"]
```

```python
from contextlib import ExitStack

import concourse.bass as bass
from concourse import mybir

ALU = mybir.AluOpType
ACT = mybir.ActivationFunctionType
F32 = mybir.dt.float32
BF16 = mybir.dt.bfloat16
I32 = mybir.dt.int32
U32 = mybir.dt.uint32
AX = mybir.AxisListType

P = 128
B, S, E = 4, 256, 256
T = B * S
NT = T // P
KC = E // P
H1, G1, D1 = 32, 8, 8
H2, D2, LAT = 16, 16, 64
HG = 4
NX, F = 8, 176
FT = (NX + 1) * F
FC = (FT + P - 1) // P
FCR = NX * F // P
FL = FT - (FC - 1) * P
PARTS = 3
Q_PART = (0, 1, 2, 0, 1, 0)
K_PART = (0, 0, 0, 1, 1, 2)
STACK = len(Q_PART)
ROWS = STACK * 16
EPS = 1e-5
RSQRT_GUESS = 0x5F3759DF
NEWTON = 3
NBANK = 8
NPLACE = 3
MISC = NBANK - 1
VBANK = 6

GROUPS = [(0, b, g) for b in range(B) for g in range(G1)] + [(1, b, g) for b in range(B) for g in range(H2 // HG)]
PER = (G1, H2 // HG)
DH = (D1, D2)
NK = (G1, H2)
NH = (H1, H2)


class Timeline:

    def __init__(self):
        self.pass1, self.pass2 = {}, {}
        self.items = {}
        self.chain = {}
        for b in range(B):
            self.add(1 + 2 * b, 1, ("k2", b))
            self.hook(2 + 2 * b, "split_k2", b)
            self.add(2 + 2 * b, 1, ("v2", b))
        ready = {(0, b): 0 for b in range(B)}
        p1 = p2 = -1
        n = 0
        while n < len(GROUPS):
            a, b, _ = GROUPS[n]
            for i in range(PER[a]):
                p1 = max(p1 + 1, ready[a, b])
                self.pass1[p1] = n + i
            self.add(p1 + 1, 1, ("neg", a, b))
            self.hook(p1 + 1, "negmax", a, b)
            p2 = max(p2, p1 + 2)
            for i in range(PER[a]):
                p2 = p2 + 1
                self.pass2[p2] = n + i
                if i % HG == HG - 1:
                    self.hook(p2 + 1, "put", n + i - HG + 1)
            s = p2 + 1
            i = B * a + b + NPLACE
            if i < 2 * B:
                self.hook(s, *(("stack_first", i) if i < B else ("stack_k2", i - B)))
            self.hook(s, "fetch", a, b)
            self.hook(s + 3, "scale", a, b)
            self.add(s + 4, 0, ("out", a, b))
            self.hook(s + 5, "norm", a + 1, b)
            self.add(s + 6, 1, ("turn", a + 1, b))
            if a == 0:
                self.add(s + 7, 1, ("q2", b))
                self.hook(s + 9, "split_q2", b)
                ready[1, b] = s + 11
            else:
                self.add(s + 7, 1, ("router", b))
                self.hook(s + 8, "gates_a", b)
                self.hook(s + 9, "gates_b", b)
                self.add(s + 10, 1, ("gates", b))
            n += PER[a]
        self.attn_steps = p2 + 2
        self.moe0 = self.attn_steps
        self.steps = self.moe0 + 2 * FC + 1

    def hook(self, s, *what):
        self.chain.setdefault(s, []).append(what)

    def add(self, s, slot, what):
        self.items.setdefault((s, slot), []).append(what)


def rsqrt_steps(dve, link, y, v, t):
    for _ in range(NEWTON):
        link(dve.scalar_tensor_tensor(out=t, in0=y, scalar=-0.5, in1=y, op0=ALU.mult, op1=ALU.mult))
        link(dve.tensor_tensor(t, t, v, ALU.mult))
        link(dve.scalar_tensor_tensor(out=y, in0=t, scalar=1.5, in1=y, op0=ALU.add, op1=ALU.mult))


def decoder_kernel(nc, x, w_first, w_small, w_latent, w_up, w_down, w_down_last, out):
    line = Timeline()
    with ExitStack() as stack:
        def sb(name, shape, dt=F32):
            return stack.enter_context(nc.sbuf_tensor(name, shape, dt))

        def sem(name):
            return stack.enter_context(nc.semaphore(name))

        def sems(name, n):
            return [sem(f"{name}{i}") for i in range(n)]

        def scratch(name, shape, dt):
            return nc.dram_tensor(name, shape, dt, kind="Internal").ap()

        q_dram = [scratch(f"q_parts{a}", (PARTS, E, T), BF16) for a in range(2)]
        k_dram = [scratch(f"k_parts{a}", (STACK, NK[a] * DH[a], T), BF16) for a in range(2)]
        o_dram = [scratch(f"o_raw{a}", (DH[a] + 1, NH[a], T), F32) for a in range(2)]

        ps = stack.enter_context(nc.psum_tensor("ps", [P, NBANK, 512], F32))
        psb = ps[:, :, :].bitcast(BF16)

        res = sb("res", [P, NT, E])
        xnT = sb("xnT", [P, KC, T])
        stats = sb("stats", [P, 4, 2, 6])
        mean_var = sb("mean_var", [P, 4, 2, 2])
        var_eps = sb("var_eps", [P, 4, 2])
        rstd = sb("rstd", [P, 4, 2])
        newton = sb("newton", [P, 4, 2])
        w_small_s = sb("w_small_s", [P, KC, 3 * E + NX])
        wo_s = [w_small_s[:, :, 0:E], w_small_s[:, :, 2 * E:3 * E]]
        wq2 = w_small_s[:, :, E:2 * E]
        gate_T = w_small_s[:, :, 3 * E:3 * E + NX]
        up_s = sb("up_s", [P, 2, KC, FT])
        down = sb("down", [P, FC, E])
        NQKV = E + 2 * G1 * D1
        shared = sb("shared", [P, 5 * 512])
        wqkv = shared[:, 0:KC * NQKV].rearrange("p (c n) -> p c n", c=KC)
        latent = shared[0:LAT, KC * NQKV:KC * NQKV + T + 2 * E]
        wkv2 = latent[:, 0:2 * E]
        ctx_T = latent[:, 2 * E:2 * E + T]
        silu = shared[:, 0:2 * 512].rearrange("p (c n) -> p c n", c=2)
        hidden = shared[:, 2 * 512:4 * 512].rearrange("p (c n) -> p c n", c=2)
        mid = shared[:, 4 * 512:5 * 512]
        ident = sb("ident", [P, P])
        identb = sb("identb", [P, P], BF16)
        mask = sb("mask", [P, P], BF16)
        ones = sb("ones", [PARTS, S], BF16)
        select = sb("select", [PARTS * NX, NX * F], BF16)
        number = sb("number", [P, NX])
        q_stack = sb("q_stack", [ROWS + PARTS, H1, NPLACE, S], BF16)
        k_stack = sb("k_stack", [ROWS + PARTS, H2, NPLACE, S], BF16)
        NPB = 2
        exact = sb("exact", [P, NPB, KC, S])
        parts = sb("parts", [P, NPB, PARTS, KC, S], BF16)
        v_s = [sb("v0", [P, NT, G1 * (D1 + 1) + 32]), sb("v1", [P, NT, H2 * (D2 + 1) + 32])]
        v_head = [v_s[a][:, :, 0:(G1, H2)[a] * (DH[a] + 1)].rearrange("p t (h d) -> p t h d", d=DH[a] + 1)
                  for a in range(2)]
        rowmax = sb("rowmax", [P, 2, 2 * H1])
        neg_rest = sb("neg_rest", [P, 2, 2 * H1])
        neg_parts = sb("neg_parts", [P, 2, PARTS, 2 * H1], BF16)
        neg_T = sb("neg_T", [H1, 2, PARTS, S], BF16)
        probs = sb("probs", [P, 2, 3, 512])
        xn_first = probs[:, :, :, :].rearrange("p a b c -> p (a b c)")[:, 0:B * 2 * E]\
            .rearrange("p (b h e) -> p b h e", b=B, h=2)
        xn = sb("xn", [P, 2, E])
        NRAW = 2 * HG
        o_raw = sb("o_raw", [P, NRAW, S])
        o_T = sb("o_T", [P, KC, S])
        r_T = sb("r_T", [P, S])
        o_tok = sb("o_tok", [P, 2, E])
        logits = sb("logits", [P, 2, NX])
        shifted = sb("shifted", [P, 2, NX])
        expd = sb("expd", [P, 2, NX])
        prob = sb("prob", [P, 2, NX])
        small = sb("small", [P, 4, 2])
        top = sb("top", [P, 2, 8])
        top_at = sb("top_at", [P, 2, 8], U32)
        top_w = sb("top_w", [P, 2, 2])
        top_f = sb("top_f", [P, 2, 2])
        gate0 = sb("gate0", [P, 2, NX])
        gate1 = sb("gate1", [P, 2, NX])
        gate_parts = sb("gate_parts", [P, 2, PARTS, NX], BF16)
        gates_T = sb("gates_T", [PARTS * NX, T], BF16)
        s_x = sems("x_loaded", B)
        s_wqkv = sem("wqkv_loaded")
        s_small = sem("small_weights_loaded")
        s_latent = sem("latent_loaded")
        s_moe = sem("expert_weights_loaded")
        s_ones = sem("ones_rows_stored")
        s_kzero = sem("k_rows_zeroed")
        s_qzero = sem("q_rows_zeroed")
        s_sel = sem("select_copied")
        s_const = sem("constants_made")
        s_xn = sem("xn_done")
        s_mm = sem("item_in_psum")
        s_item = sem("item_copied_out")
        s_split = [sem("split_by_vector"), sem("split_by_pool")]
        s_parts_out = sems("parts_stored", NPB)
        s_qst = [sems("q0_stacked", B), sems("q1_stacked", B)]
        s_kst = [sems("k0_stacked", B), sems("k1_stacked", B)]
        s_p1 = sem("scores_for_max")
        s_max = sem("maxima_done")
        s_neg = sem("negmax_parts")
        s_nst = [sems("neg0_stacked", B), sems("neg1_stacked", B)]
        s_p2 = sem("scores_for_exp")
        s_exp = sem("exp_done")
        s_keep = sem("masked")
        s_pv = sem("pv_done")
        s_raw = sem("o_raw_copied")
        s_put = sems("o_raw_stored", len(GROUPS) // HG)
        s_vones = sem("v_ones_set")
        s_oT = sem("o_T_loaded")
        s_rT = sem("sums_loaded")
        s_scaled = sem("oT_scaled")
        s_ga = sem("logits_shifted")
        s_gexp = sem("router_exp")
        s_gp = sem("gate_parts_done")
        s_g = sem("gate_proj")
        s_u = sem("up_proj")
        s_e = sem("gates_spread")
        s_silu = sem("silu_done")
        s_h = sem("hidden_done")
        s_down = sem("down_done")
        s_y = sem("result_done")
        s_out = sem("result_stored")
        seq_v = sem("vector_sequence")
        seq_p = sem("pool_sequence")

        def linker(eng, s):
            count = [0]

            def link(ins, n=1):
                count[0] += n
                ins.then_inc(s, n)
                eng.wait_ge(s, count[0])
                return ins

            return link

        first = []
        for b in range(B):
            first += [("turn", 0, b), ("q1", b), ("k1", b), ("v1", b)]
        later = []
        for s in range(line.steps):
            later += line.items.get((s, 0), []) + line.items.get((s, 1), [])
        number_of = {it: k for k, it in enumerate(first + later)}
        pieces = [it for it in first + later if it[0] in ("q1", "k1", "q2", "k2")]
        piece_of = {p: i for i, p in enumerate(pieces)}
        splitter = [1 if p[0] == "k2" else 0 for p in pieces]
        split_no = [splitter[:i + 1].count(splitter[i]) for i in range(len(pieces))]
        n_stores = {"q1": KC, "q2": KC, "k1": PARTS, "k2": PARTS * KC}

        def stores_until(i):
            return sum(n_stores[pieces[k][0]] for k in range(i % NPB, i + 1, NPB))

        def chains(kind):
            found = [w[1:] for s in range(line.steps) for w in line.chain.get(s, []) if w[0] == kind]
            return {w: i for i, w in enumerate(found)}

        order = {k: chains(k) for k in ("negmax", "scale", "gates_a", "gates_b")}
        norm_of = {(0, b): b for b in range(B)} | {w: B + i for w, i in chains("norm").items()}
        NORM_ORDER = {k: ab for ab, k in norm_of.items()}
        last_group = {GROUPS[n][:2]: n for n in range(len(GROUPS))}

        def head_slots(n):
            a, _, g = GROUPS[n]
            return slice(g, H1, G1) if a == 0 else slice(HG * g, HG * g + HG)

        def place_of(a, b):
            return (B * a + b) % NPLACE

        block = stack.enter_context(nc.Block())

        @block.sync
        def _(sp):
            for b in range(B):
                sp.dma_start(res[:, 2 * b:2 * b + 2, :], x[b].rearrange("(h p) e -> p h e", p=P)).then_inc(s_x[b], 16)
            sp.dma_start(wqkv[:, :, :], w_first).then_inc(s_wqkv, 16)
            sp.dma_start(latent[:, :], w_latent).then_inc(s_latent, 16)
            sp.wait_ge(s_const, 1)
            for place in range(NPLACE):
                sp.dma_start(k_stack[ROWS:ROWS + PARTS, :, place, :],
                             ones[:, None, :].to_broadcast([PARTS, H2, S])).then_inc(s_ones, 16)
            for p in range(1, PARTS):
                sp.dma_start(select[NX * p:NX * p + NX, :], select[0:NX, :]).then_inc(s_sel, 16)

            def store_parts(piece):
                kind, b = piece
                i = piece_of[piece]
                a = 0 if kind in ("q1", "k1") else 1
                dram = (q_dram if kind[0] == "q" else k_dram)[a]
                rows = min(P, dram.shape[1])
                buf = i % NPB
                sp.wait_ge(s_split[splitter[i]], split_no[i])
                for c in range(dram.shape[1] // rows):
                    dst = dram[:, rows * c:rows * c + rows, b * S:b * S + S].rearrange("j r t -> r j t")
                    if kind[0] == "q":
                        sp.dma_start(dst, parts[:, buf, :, c, :]).then_inc(s_parts_out[buf], 16)
                        continue
                    for part in range(PARTS):
                        slots = [j for j in range(STACK) if K_PART[j] == part]
                        sp.dma_start(dst[:, slots[0]:slots[-1] + 1, :],
                                     parts[0:rows, buf, part, c, :][:, None, :].to_broadcast([rows, len(slots), S]))\
                          .then_inc(s_parts_out[buf], 16)

            def stored(piece):
                i = piece_of[piece]
                sp.wait_ge(s_parts_out[i % NPB], 16 * stores_until(i))

            def place_free(a, b):
                i = B * a + b - NPLACE
                if i >= 0:
                    sp.wait_ge(s_p2, 2 * last_group[i // B, i % B] + 2)

            def load_q(a, b):
                d = DH[a]
                tok = slice(b * S, b * S + S)
                r = 0
                for n in range(PARTS, 0, -1):
                    sp.dma_start(q_stack[r:r + n * d, 0:NH[a], place_of(a, b), :],
                                 q_dram[a][0:n, :, tok].rearrange("j (d h) t -> (j d) h t", d=d))\
                      .then_inc(s_qst[a][b], 16)
                    r += n * d

            def load_k(a, b):
                d = DH[a]
                sp.dma_start(k_stack[0:STACK * d, 0:NK[a], place_of(a, b), :],
                             k_dram[a][:, :, b * S:b * S + S].rearrange("j (d h) t -> (j d) h t", d=d))\
                  .then_inc(s_kst[a][b], 16)

            def stack_first(b):
                stored(("q1", b))
                place_free(0, b)
                load_q(0, b)
                stored(("k1", b))
                load_k(0, b)

            sp.wait_ge(s_kzero, 2)
            for b in range(B):
                store_parts(("q1", b))
                store_parts(("k1", b))
                if b < NPLACE:
                    sp.wait_ge(s_qzero, 2 * (b + 1))
                    stack_first(b)
                if b == 0:
                    sp.dma_start(w_small_s[:, :, :], w_small).then_inc(s_small, 16)

            for s in range(line.steps):
                for what, *arg in line.chain.get(s, []):
                    if what == "stack_first":
                        stack_first(*arg)
                    if what == "stack_k2":
                        b, = arg
                        stored(("k2", b))
                        place_free(1, b)
                        load_k(1, b)
                    if what == "split_k2":
                        b, = arg
                        store_parts(("k2", b))
                        if b == 0:
                            for w in range(2):
                                sp.dma_start(up_s[:, w, :, :], w_up[:, w, :, :]).then_inc(s_moe, 16)
                            sp.dma_start(down[:, 0:FC - 1, :], w_down).then_inc(s_moe, 16)
                            sp.dma_start(down[0:FL, FC - 1, :], w_down_last).then_inc(s_moe, 16)
                    if what == "put":
                        n0, = arg
                        a, b, g0 = GROUPS[n0]
                        d = DH[a]
                        tok = slice(b * S, b * S + S)
                        sp.wait_ge(s_raw, n0 + HG)
                        for j in range(HG):
                            hs = slice(G1 * j + g0, G1 * j + g0 + HG) if a == 0 else slice(j, H2, HG)
                            sp.dma_start(o_dram[a][:, hs, tok],
                                         o_raw[32 * j:32 * j + d + 1, n0 % NRAW:n0 % NRAW + HG, :])\
                              .then_inc(s_put[n0 // HG], 16)
                    if what == "negmax":
                        a, b = arg
                        i = order["negmax"][a, b]
                        sp.wait_ge(s_item, number_of["neg", a, b] + 1)
                        for p in range(PARTS):
                            sp.dma_start(q_stack[ROWS + p:ROWS + p + 1, 0:NH[a], place_of(a, b), :],
                                         neg_T[0:NH[a], i % 2, p, :]).then_inc(s_nst[a][b], 16)
                    if what == "fetch":
                        a, b = arg
                        i = order["scale"][a, b]
                        d = DH[a]
                        tok = slice(b * S, b * S + S)
                        for n0 in range(last_group[a, b] + 1 - PER[a], last_group[a, b], HG):
                            sp.wait_ge(s_put[n0 // HG], 16 * HG)
                        if i >= 1:
                            sp.wait_ge(s_scaled, i)
                            sp.wait_ge(s_mm, number_of["out", (i - 1) // B, (i - 1) % B] + 1)
                        sp.dma_start(r_T[:, :], o_dram[a][d:d + 1, :, tok].to_broadcast([d // KC, NH[a], S]))\
                          .then_inc(s_rT, 16)
                        sp.dma_start(o_T[:, :, :], o_dram[a][0:d, :, tok].rearrange("(c d) h t -> (d h) c t", c=KC))\
                          .then_inc(s_oT, 16)
                    if what == "split_q2":
                        b, = arg
                        store_parts(("q2", b))
                        stored(("q2", b))
                        place_free(1, b)
                        load_q(1, b)
                if s in (line.moe0 + FC, line.moe0 + 2 * FC):
                    hf = 0 if s == line.moe0 + FC else 1
                    for k in range(2):
                        sp.wait_ge(s_y, 2 * hf + k + 1)
                        sp.dma_start(out[2 * hf + k].rearrange("(h p) e -> p h e", p=P),
                                     res[:, 4 * hf + 2 * k:4 * hf + 2 * k + 2, :]).then_inc(s_out, 16)
            sp.wait_ge(s_out, 16 * B)

        def split(eng, link, piece):
            i = piece_of[piece]
            rows, chunks = (G1 * D1, 1) if piece[0] == "k1" else (P, KC)
            hi, mid_, lo = (parts[0:rows, i % NPB, j, 0:chunks, :] for j in range(PARTS))
            r = exact[0:rows, i % NPB, 0:chunks, :]
            eng.wait_ge(s_item, number_of[piece] + 1)
            link(eng.tensor_tensor(r, r, hi, ALU.subtract))
            link(eng.tensor_copy(mid_, r))
            eng.tensor_tensor(lo, r, mid_, ALU.subtract).then_inc(s_split[splitter[i]], 1)

        @block.gpsimd
        def _(pool):
            link = linker(pool, seq_p)
            pool.memset(v_s[0][:, :, :], 1.0).then_inc(s_vones, 1)
            pool.memset(v_s[1][:, :, :], 1.0).then_inc(s_vones, 1)
            pool.memset(ones[:, :], 1.0)
            link(pool.memset(mask[:, :], 0.0))
            link(pool.memset(select[0:NX, :], 1.0))
            for k, r in enumerate((32, 64)):
                pool.memset(k_stack[r:r + 32, 0:G1, :, :].bitcast(U32), 0).then_inc(s_kzero, 1)
                pool.wait_ge(s_kzero, k + 1)
            for e in range(NX):
                pool.memset(number[:, e:e + 1], float(e))
            link(pool.memset(ident[:, :], 0.0))
            link(pool.affine_select(out=ident[:, :], in_=ident[:, :], compare_op=ALU.not_equal, fill=1.0, base=0,
                                    pattern=[[-1, P]], channel_multiplier=1))
            pool.tensor_copy(identb[:, :], ident[:, :])
            pool.affine_select(out=mask[:, :], in_=mask[:, :], compare_op=ALU.is_ge, fill=-1e30, base=0,
                               pattern=[[-1, P]], channel_multiplier=1)
            link(pool.affine_select(out=select[0:NX, :], in_=select[0:NX, :], compare_op=ALU.is_ge, fill=0.0,
                                    base=0, pattern=[[1, NX * F]], channel_multiplier=-F))
            pool.affine_select(out=select[0:NX, :], in_=select[0:NX, :], compare_op=ALU.is_ge, fill=0.0,
                               base=F - 1, pattern=[[-1, NX * F]], channel_multiplier=F).then_inc(s_const, 1)

            for place in range(NPLACE):
                for k, r in enumerate((32, 64)):
                    pool.memset(q_stack[r:r + 32, :, place, :].bitcast(U32), 0).then_inc(s_qzero, 1)
                    pool.wait_ge(s_qzero, 2 * place + k + 1)
            for s in range(line.steps):
                if s in line.pass2:
                    n = line.pass2[s]
                    for u, count in ((0, 2 * n + 1), (2, 2 * n + 2)):
                        blk = probs[:, n % 2, u, :].rearrange("p (h q) -> p h q", h=HG)
                        pool.wait_ge(s_exp, count)
                        pool.affine_select(out=blk, in_=blk, compare_op=ALU.is_ge, fill=0.0, base=0,
                                           pattern=[[0, HG], [1, P]], channel_multiplier=-1).then_inc(s_keep, 1)
                for what, *arg in line.chain.get(s, []):
                    if what == "split_k2":
                        split(pool, link, ("k2", *arg))

        @block.scalar
        def _(act):
            def copy(dst, src, scale=None):
                return act.activation(dst, src, ACT.Copy, scale=scale) if scale else act.copy(dst, src)

            def copy_item(it):
                k = number_of[it]
                bank = k % NBANK if k < len(first) else MISC
                act.wait_ge(s_mm, k + 1)
                kind = it[0]
                if kind == "turn":
                    b = it[2]
                    last = copy(xnT[:, :, b * S:b * S + S], ps[:, bank, :].rearrange("p (c t) -> p c t", c=KC))
                elif kind in ("q1", "q2", "k1", "k2"):
                    i = piece_of[it]
                    buf = i % NPB
                    rows, chunks = (G1 * D1, 1) if kind == "k1" else (P, KC)
                    scale = {"q1": D1 ** -0.5, "q2": D2 ** -0.5}.get(kind)
                    if i >= NPB:
                        j = i - NPB
                        act.wait_ge(s_split[splitter[j]], split_no[j])
                        act.wait_ge(s_parts_out[buf], 16 * stores_until(j))
                    src = ps[0:rows, bank, 0:chunks * S].rearrange("p (c t) -> p c t", c=chunks)
                    copy(exact[0:rows, buf, 0:chunks, :], src, scale)
                    last = copy(parts[0:rows, buf, 0, 0:chunks, :], src, scale)
                elif kind == "v1":
                    b = it[1]
                    act.wait_ge(s_vones, 1)
                    last = copy(v_head[0][:, 2 * b:2 * b + 2, :, 0:D1],
                                ps[:, bank, 0:2 * G1 * D1].rearrange("p (t g d) -> p t g d", t=2, d=D1))
                elif kind == "v2":
                    b = it[1]
                    act.wait_ge(s_vones, 2)
                    last = copy(v_head[1][:, 2 * b:2 * b + 2, :, 0:D2],
                                ps[:, bank, :].rearrange("p (t h d) -> p t h d", t=2, d=D2))
                elif kind == "neg":
                    a, b = it[1:]
                    i = order["negmax"][a, b]
                    if i >= 2:
                        a0, b0 = (i - 2) // B, (i - 2) % B
                        act.wait_ge(s_nst[a0][b0], 16 * PARTS)
                    last = copy(neg_T[0:NH[a], i % 2, :, :],
                                psb[0:NH[a], bank, 0:PARTS * S].rearrange("p (j t) -> p j t", j=PARTS))
                elif kind == "out":
                    last = copy(o_tok[:, :, :], ps[:, bank, :].rearrange("p (h e) -> p h e", h=2))
                elif kind == "router":
                    last = copy(logits[:, :, :], ps[:, bank, 0:2 * NX].rearrange("p (t e) -> p t e", t=2))
                else:
                    b = it[1]
                    last = copy(gates_T[:, b * S:b * S + S], psb[0:PARTS * NX, bank, 0:S])
                last.then_inc(s_item, 1)

            for it in first:
                copy_item(it)
            for s in range(line.steps):
                for it in line.items.get((s, 0), []):
                    copy_item(it)
                n = line.pass2.get(s)
                if n is not None:
                    act.wait_ge(s_p2, 2 * n + 1)
                    if n >= 2:
                        act.wait_ge(s_pv, n - 1)
                    act.activation(probs[:, n % 2, 0, :], ps[:, 3, :], ACT.Exp).then_inc(s_exp, 1)
                before = line.pass2.get(s - 1)
                if before is not None:
                    act.wait_ge(s_pv, before + 1)
                    if before >= NRAW:
                        act.wait_ge(s_put[(before - NRAW) // HG], 16 * HG)
                    copy(o_raw[:, before % NRAW, :], ps[:, VBANK, 0:S]).then_inc(s_raw, 1)
                for it in line.items.get((s, 1), []):
                    copy_item(it)
                if n is not None:
                    act.wait_ge(s_p2, 2 * n + 2)
                    act.activation(probs[:, n % 2, 1:3, :], ps[:, 4:6, :], ACT.Exp).then_inc(s_exp, 1)
                c = s - line.moe0
                if 0 <= c < 2 * FC:
                    rows = FL if c % FC == FC - 1 else P
                    act.wait_ge(s_g, c + 1)
                    if c >= 2:
                        act.wait_ge(s_h, c - 1)
                    act.activation(silu[0:rows, c % 2, :], ps[0:rows, c % 2, :], ACT.Silu).then_inc(s_silu, 1)
                for what, *arg in line.chain.get(s, []):
                    if what == "gates_a":
                        act.wait_ge(s_ga, order["gates_a"][tuple(arg)] + 1)
                        act.activation(expd[:, :, :], shifted[:, :, :], ACT.Exp).then_inc(s_gexp, 1)

        @block.vector
        def _(dve):
            link = linker(dve, seq_v)

            def variance(k, b):
                for h in range(2):
                    last = dve.bn_stats(stats[:, k % 4, h, :], res[:, 2 * b + h, :])
                link(last)
                for h in range(2):
                    last = dve.bn_aggr(mean_var[:, k % 4, h, :], stats[:, k % 4, h, :])
                link(last)
                link(dve.tensor_scalar(var_eps[:, k % 4, :], mean_var[:, k % 4, :, 1], EPS, None, ALU.add))

            def rsqrt(k0, k1):
                v, y, t = (z[:, k0:k1, :] for z in (var_eps, rstd, newton))
                link(dve.tensor_scalar(y.bitcast(I32), v.bitcast(I32), 1, None, ALU.arith_shift_right))
                link(dve.tensor_scalar(y.bitcast(I32), y.bitcast(I32), -1, RSQRT_GUESS, ALU.mult, ALU.add))
                rsqrt_steps(dve, link, y, v, t)

            def normed(k, b, dst):
                for h in range(2):
                    last = dve.tensor_scalar(dst[:, h, :], res[:, 2 * b + h, :], mean_var[:, k % 4, h, 0:1],
                                             rstd[:, k % 4, h:h + 1], ALU.subtract, ALU.mult)
                last.then_inc(s_xn, 1)

            def gates(b):
                i = order["gates_b"][b,]
                total, inv, den, rden = (small[:, k, :] for k in range(4))
                dve.wait_ge(s_gexp, i + 1)
                link(dve.tensor_reduce(total, expd[:, :, :], AX.X, ALU.add))
                link(dve.reciprocal(inv, total))
                link(dve.tensor_tensor(prob[:, :, :], expd[:, :, :], inv[:, :, None].to_broadcast([P, 2, NX]),
                                       ALU.mult))
                for h in range(2):
                    link(dve.max(top[:, h, :], prob[:, h, :]))
                for h in range(2):
                    link(dve.max_index(top_at[:, h, :], top[:, h, :], prob[:, h, :]))
                link(dve.tensor_copy(top_f[:, :, :], top_at[:, :, 0:2]))
                link(dve.tensor_tensor(den, top[:, :, 0], top[:, :, 1], ALU.add))
                link(dve.reciprocal(rden, den))
                link(dve.tensor_tensor(top_w[:, :, :], top[:, :, 0:2], rden[:, :, None].to_broadcast([P, 2, 2]),
                                       ALU.mult))
                for h in range(2):
                    for k, gate in enumerate((gate0, gate1)):
                        link(dve.tensor_scalar(gate[:, h, :], number[:, :], top_f[:, h, k:k + 1],
                                               top_w[:, h, k:k + 1], ALU.is_equal, ALU.mult))
                link(dve.tensor_tensor(gate0[:, :, :], gate0[:, :, :], gate1[:, :, :], ALU.add))
                hi, mi, lo = (gate_parts[:, :, j, :] for j in range(PARTS))
                link(dve.tensor_copy(hi, gate0[:, :, :]))
                link(dve.tensor_tensor(gate1[:, :, :], gate0[:, :, :], hi, ALU.subtract))
                link(dve.tensor_copy(mi, gate1[:, :, :]))
                dve.tensor_tensor(lo, gate1[:, :, :], mi, ALU.subtract).then_inc(s_gp, 1)

            for b in range(B):
                dve.wait_ge(s_x[b], 16)
                variance(b, b)
            rsqrt(0, B)
            for b in range(B):
                normed(b, b, xn_first[:, b])
            for b in range(B):
                split(dve, link, ("q1", b))
                split(dve, link, ("k1", b))

            for s in range(line.steps):
                for what, *arg in line.chain.get(s, []):
                    if what == "negmax":
                        a, b = arg
                        i = order["negmax"][a, b]
                        w = 2 * NH[a]
                        m, r = rowmax[:, i % 2, 0:w], neg_rest[:, i % 2, 0:w]
                        hi, mi, lo = (neg_parts[:, i % 2, j, 0:w] for j in range(PARTS))
                        dve.wait_ge(s_max, 2 * last_group[a, b] + 2)
                        link(dve.tensor_scalar(m, m, -1.0, None, ALU.mult))
                        link(dve.tensor_copy(hi, m))
                        link(dve.tensor_tensor(r, m, hi, ALU.subtract))
                        link(dve.tensor_copy(mi, r))
                        dve.tensor_tensor(lo, r, mi, ALU.subtract).then_inc(s_neg, 1)
                    if what == "scale":
                        a, b = arg
                        i = order["scale"][a, b]
                        dve.wait_ge(s_rT, 16 * (i + 1))
                        link(dve.reciprocal(r_T[:, :], r_T[:, :]))
                        dve.wait_ge(s_oT, 16 * (i + 1))
                        dve.tensor_tensor(o_T[:, :, :], o_T[:, :, :], r_T[:, None, :].to_broadcast([P, KC, S]),
                                          ALU.mult).then_inc(s_scaled, 1)
                    if what == "split_q2":
                        split(dve, link, ("q2", *arg))
                    if what == "norm":
                        a, b = arg
                        k = norm_of[a, b]
                        dve.wait_ge(s_item, number_of["out", a - 1, b] + 1)
                        tiles = res[:, 2 * b:2 * b + 2, :]
                        link(dve.tensor_tensor(tiles, tiles, o_tok[:, :, :], ALU.add))
                        variance(k, b)
                        rsqrt(k % 4, k % 4 + 1)
                        if k > B:
                            dve.wait_ge(s_mm, number_of[("turn",) + NORM_ORDER[k - 1]] + 1)
                        normed(k, b, xn)
                    if what == "gates_a":
                        b, = arg
                        dve.wait_ge(s_item, number_of["router", b] + 1)
                        link(dve.tensor_reduce(small[:, 0, :], logits[:, :, :], AX.X, ALU.max))
                        dve.tensor_tensor(shifted[:, :, :], logits[:, :, :],
                                          small[:, 0, :, None].to_broadcast([P, 2, NX]), ALU.subtract)\
                            .then_inc(s_ga, 1)
                    if what == "gates_b":
                        gates(*arg)
                n = line.pass1.get(s)
                if n is not None:
                    a, b, g = GROUPS[n]
                    i = order["negmax"][a, b]
                    m = rowmax[:, i % 2, :]
                    hs = head_slots(n)
                    dve.wait_ge(s_p1, 2 * n + 1)
                    dve.tensor_reduce(m[:, 0:NH[a]][:, hs], ps[:, 0, :].rearrange("p (h k) -> p h k", h=HG),
                                      AX.X, ALU.max).then_inc(s_max, 1)
                    dve.wait_ge(s_p1, 2 * n + 2)
                    dve.tensor_reduce(m[:, NH[a]:2 * NH[a]][:, hs],
                                      ps[:, 1:3, :].rearrange("p u (h k) -> p h u k", h=HG),
                                      AX.XY, ALU.max).then_inc(s_max, 1)
                c = s - line.moe0
                if 0 <= c < 2 * FC:
                    fc = c % FC
                    rows = FL if fc == FC - 1 else P
                    dve.wait_ge(s_silu, c + 1)
                    dve.wait_ge(s_u, c + 1)
                    if c >= 2:
                        dve.wait_ge(s_down, c - 1)
                    if c >= 1:
                        dve.wait_ge(s_h, c)
                    if fc < FCR:
                        link(dve.tensor_tensor(mid[:, :], silu[:, c % 2, :], ps[:, 2 + c % 2, :], ALU.mult))
                        dve.wait_ge(s_e, FCR * (c // FC) + fc + 1)
                        dve.tensor_tensor(hidden[:, c % 2, :], mid[:, :], ps[:, 4, :], ALU.mult).then_inc(s_h, 1)
                    else:
                        dve.tensor_tensor(hidden[0:rows, c % 2, :], silu[0:rows, c % 2, :],
                                          ps[0:rows, 2 + c % 2, :], ALU.mult).then_inc(s_h, 1)
                if c in (FC, 2 * FC):
                    hf = c // FC - 1
                    dve.wait_ge(s_down, FC * (hf + 1))
                    for k in range(2):
                        tiles = res[:, 4 * hf + 2 * k:4 * hf + 2 * k + 2, :]
                        dve.tensor_tensor(tiles, ps[:, 5 + k, :].rearrange("p (t e) -> p t e", t=2), tiles,
                                          ALU.add).then_inc(s_y, 1)

        @block.tensor
        def _(pe):
            def mm(dst, lhsT, rhs, start=True, stop=True):
                return pe.matmul(dst, lhsT, rhs, start=start, stop=stop)

            def item(it):
                k = number_of[it]
                bank = k % NBANK if k < len(first) else MISC
                if k >= len(first):
                    pe.wait_ge(s_item, k)
                elif k >= NBANK:
                    pe.wait_ge(s_item, k - NBANK + 1)
                kind = it[0]
                dst = ps[:, bank, :]
                if kind == "turn":
                    _, a, b = it
                    src = xn_first[:, b] if a == 0 else xn
                    pe.wait_ge(s_xn, norm_of[a, b] + 1)
                    for h in range(2):
                        for c in range(KC):
                            last = pe.transpose(dst[:, S * c + P * h:S * c + P * h + P], src[:, h, P * c:P * c + P],
                                                ident[:, :])
                elif kind in ("q1", "q2", "k1"):
                    b = it[1]
                    pe.wait_ge(s_item, number_of["turn", 1 if kind == "q2" else 0, b] + 1)
                    w, m, c0 = {"q1": (wqkv, P, 0), "k1": (wqkv, G1 * D1, E), "q2": (wq2, P, 0)}[kind]
                    for n in range(1 if kind == "k1" else KC):
                        for c in range(KC):
                            last = mm(dst[0:m, S * n:S * n + S], w[:, c, c0 + m * n:c0 + m * n + m],
                                      xnT[:, c, b * S:b * S + S], c == 0, c == KC - 1)
                elif kind == "v1":
                    b = it[1]
                    w = G1 * D1
                    for h in range(2):
                        t = 2 * b + h
                        for c in range(KC):
                            last = mm(dst[:, w * h:w * h + w], xnT[:, c, P * t:P * t + P],
                                      wqkv[:, c, E + w:E + 2 * w], c == 0, c == KC - 1)
                elif kind == "k2":
                    b = it[1]
                    for c in range(KC):
                        last = mm(dst[:, S * c:S * c + S], wkv2[:, P * c:P * c + P], ctx_T[:, b * S:b * S + S])
                elif kind == "v2":
                    b = it[1]
                    for h in range(2):
                        t = 2 * b + h
                        last = mm(dst[:, E * h:E * h + E], ctx_T[:, P * t:P * t + P], wkv2[:, E:2 * E])
                elif kind == "neg":
                    _, a, b = it
                    i = order["negmax"][a, b]
                    w = NH[a]
                    pe.wait_ge(s_neg, i + 1)
                    for j in range(PARTS):
                        for qb in range(2):
                            last = pe.transpose(psb[0:w, bank, S * j + P * qb:S * j + P * qb + P],
                                                neg_parts[:, i % 2, j, w * qb:w * qb + w], identb[:, :])
                elif kind == "out":
                    _, a, b = it
                    pe.wait_ge(s_scaled, order["scale"][a, b] + 1)
                    for h in range(2):
                        for c in range(KC):
                            last = mm(dst[:, E * h:E * h + E], o_T[:, c, P * h:P * h + P], wo_s[a][:, c, :],
                                      c == 0, c == KC - 1)
                elif kind == "router":
                    b = it[1]
                    pe.wait_ge(s_item, number_of["turn", 2, b] + 1)
                    for h in range(2):
                        t = 2 * b + h
                        for c in range(KC):
                            last = mm(dst[:, NX * h:NX * h + NX], xnT[:, c, P * t:P * t + P], gate_T[:, c, :],
                                      c == 0, c == KC - 1)
                else:
                    b = it[1]
                    pe.wait_ge(s_gp, order["gates_b"][b,] + 1)
                    for h in range(2):
                        last = pe.transpose(psb[0:PARTS * NX, bank, P * h:P * h + P],
                                            gate_parts[:, h, :, :].rearrange("p j e -> p (j e)"), identb[:, :])
                last.then_inc(s_mm, 1)

            def scores_max(n, blocks):
                a, b, g = GROUPS[n]
                rows = ROWS
                place = place_of(a, b)
                heads = range(H1)[head_slots(n)]
                for bank, qb, kb in blocks:
                    if qb == kb:
                        mm(ps[:, bank, :], identb[:, :], mask[:, None, :].to_broadcast([P, HG, P]), True, False)
                    for j, h in enumerate(heads):
                        last = mm(ps[:, bank, P * j:P * j + P],
                                  q_stack[0:rows, h, place, P * qb:P * qb + P],
                                  k_stack[0:rows, g if a == 0 else h, place, P * kb:P * kb + P],
                                  qb != kb, qb != kb or j == HG - 1)
                last.then_inc(s_p1, 1)

            def scores_exp(n, blocks):
                a, b, g = GROUPS[n]
                rows = ROWS + PARTS
                place = place_of(a, b)
                for bank, qb, kb in blocks:
                    q = q_stack[0:rows, head_slots(n), place, P * qb:P * qb + P]
                    if a == 0:
                        last = mm(ps[:, bank, :], k_stack[0:rows, g, place, P * kb:P * kb + P], q)
                        continue
                    for j, h in enumerate(range(H1)[head_slots(n)]):
                        last = mm(ps[:, bank, P * j:P * j + P], k_stack[0:rows, h, place, P * kb:P * kb + P],
                                  q_stack[0:rows, h, place, P * qb:P * qb + P])
                last.then_inc(s_p2, 1)

            def weigh(n):
                a, b, g = GROUPS[n]
                d = DH[a] + 1
                pe.wait_ge(s_keep, 2 * n + 2)
                if n >= 1:
                    pe.wait_ge(s_raw, n)
                heads = [g if a == 0 else h for h in range(H1)[head_slots(n)]]
                for kb in range(2):
                    for j, h in enumerate(heads):
                        last = mm(ps[32 * j:32 * j + 32, VBANK, P * kb:S],
                                  v_s[a][:, 2 * b + kb, d * h:d * h + 32],
                                  probs[:, n % 2, 2 * kb:2, P * j:P * j + P] if kb == 0 else
                                  probs[:, n % 2, 2, P * j:P * j + P], kb == 0, kb == 1)
                last.then_inc(s_pv, 1)

            pe.wait_ge(s_const, 1)
            pe.wait_ge(s_wqkv, 16)
            for it in first:
                item(it)
            pe.wait_ge(s_item, len(first))
            pe.wait_ge(s_ones, 16 * NPLACE)
            pe.wait_ge(s_latent, 16)
            pe.wait_ge(s_small, 16)
            for s in range(line.steps):
                for it in line.items.get((s, 0), []):
                    item(it)
                m, n, before = line.pass1.get(s), line.pass2.get(s), line.pass2.get(s - 1)
                if m is not None:
                    a, b, g = GROUPS[m]
                    if g == 0:
                        pe.wait_ge(s_qst[a][b], 16 * PARTS)
                        pe.wait_ge(s_kst[a][b], 16)
                    if m >= 1:
                        pe.wait_ge(s_max, 2 * m - 1)
                    scores_max(m, [(0, 0, 0)])
                if n is not None:
                    a, b, g = GROUPS[n]
                    if g == 0:
                        pe.wait_ge(s_nst[a][b], 16 * PARTS)
                    if n >= 1:
                        pe.wait_ge(s_exp, 2 * n - 1)
                    scores_exp(n, [(3, 0, 0)])
                if before is not None:
                    weigh(before)
                for it in line.items.get((s, 1), []):
                    item(it)
                if m is not None:
                    if m >= 1:
                        pe.wait_ge(s_max, 2 * m)
                    scores_max(m, [(1, 1, 0), (2, 1, 1)])
                if n is not None:
                    if n >= 1:
                        pe.wait_ge(s_exp, 2 * n)
                    scores_exp(n, [(4, 1, 0), (5, 1, 1)])
                c = s - line.moe0
                if c == 0:
                    pe.wait_ge(s_raw, len(GROUPS))
                    pe.wait_ge(s_moe, 16 * 4)
                    pe.wait_ge(s_sel, 16 * (PARTS - 1))
                if 0 <= c < 2 * FC:
                    hf, fc = divmod(c, FC)
                    m = FL if fc == FC - 1 else P
                    if fc == 0:
                        pe.wait_ge(s_item, number_of["gates", 2 * hf + 1] + 1)
                    tok = slice(512 * hf, 512 * hf + 512)
                    if c >= 2:
                        pe.wait_ge(s_h, c - 1)
                    for w, bank, done in ((up_s[:, 0], 0, s_g), (up_s[:, 1], 2, s_u)):
                        for k in range(KC):
                            last = mm(ps[0:m, bank + c % 2, :], w[:, k, P * fc:P * fc + m], xnT[:, k, tok],
                                      k == 0, k == KC - 1)
                        last.then_inc(done, 1)
                    if fc < FCR:
                        if c >= 1:
                            pe.wait_ge(s_h, c)
                        mm(ps[:, 4, :], select[:, P * fc:P * fc + P], gates_T[:, tok]).then_inc(s_e, 1)
                if 1 <= c <= 2 * FC:
                    hf, fc = divmod(c - 1, FC)
                    r = FL if fc == FC - 1 else P
                    pe.wait_ge(s_h, c)
                    if fc == 0 and hf == 1:
                        pe.wait_ge(s_y, 2)
                    for t in range(4):
                        last = pe.matmul(ps[:, 5 + t // 2, E * (t % 2):E * (t % 2) + E],
                                         hidden[0:r, (c - 1) % 2, P * t:P * t + P], down[0:r, fc, :],
                                         start=fc == 0 and t % 2 == 0, stop=fc == FC - 1,
                                         skip_group_check=True)
                    last.then_inc(s_down, 1)


def by_dim(w, heads):
    return w.reshape(w.shape[0], heads, -1).transpose(0, 2, 1).reshape(w.shape[0], -1)


def rows_on_partitions(w):
    return w.reshape(-1, P, w.shape[1]).transpose(1, 0, 2)


def kernel(x, ctx_512, L0_attn_Wq, L0_attn_Wk, L0_attn_Wv, L0_attn_Wo, L0_xattn_Wq, L0_xattn_Wkv_expand,
           L0_xattn_Wout, L0_ffn_gate_w, L0_ffn_w_gate, L0_ffn_w_up, L0_ffn_w_down, L0_ffn_sw_gate, L0_ffn_sw_up,
           L0_ffn_sw_down):
    import numpy as np
    import concourse.bacc as bacc
    from concourse.bass_utils import run_bass_kernel_spmd

    (x, ctx, wq, wk, wv, wo, xwq, xwkv, xwo, gate_w, w_gate, w_up, w_down, sw_gate, sw_up, sw_down) = (
        np.asarray(a) for a in (
            x, ctx_512, L0_attn_Wq, L0_attn_Wk, L0_attn_Wv, L0_attn_Wo, L0_xattn_Wq, L0_xattn_Wkv_expand,
            L0_xattn_Wout, L0_ffn_gate_w, L0_ffn_w_gate, L0_ffn_w_up, L0_ffn_w_down, L0_ffn_sw_gate, L0_ffn_sw_up,
            L0_ffn_sw_down))
    first = np.concatenate([by_dim(wq, H1), by_dim(wk, G1), wv], 1)
    small = np.concatenate([by_dim(wo.T, H1).T, by_dim(xwq.T, H2), by_dim(xwo, H2).T, gate_w.T], 1)
    latent = np.concatenate([by_dim(xwkv[0:E].T, H2), xwkv[E:2 * E].T, ctx.reshape(T, LAT).T], 1)
    ups = [np.concatenate([w.transpose(1, 0, 2).reshape(E, NX * F), one], 1)
           for w, one in ((w_gate, sw_gate), (w_up, sw_up))]
    downs = np.concatenate([w_down.reshape(NX * F, E), sw_down], 0)
    cut = (FC - 1) * P
    arrays = {
        "x": x,
        "w_first": rows_on_partitions(first),
        "w_small": rows_on_partitions(small),
        "w_latent": latent,
        "w_up": np.stack([rows_on_partitions(w) for w in ups], 1),
        "w_down": rows_on_partitions(downs[0:cut]),
        "w_down_last": downs[cut:FT],
    }
    nc = bacc.Bacc("TRN2", target_bir_lowering=False, num_devices=1)
    given, args = {}, []
    for name, a in arrays.items():
        given[f"in_{name}"] = a = np.ascontiguousarray(a)
        args.append(nc.dram_tensor(f"in_{name}", a.shape, mybir.dt.from_np(a.dtype), kind="ExternalInput").ap())
    args.append(nc.dram_tensor("out", (B, S, E), F32, kind="ExternalOutput").ap())
    decoder_kernel(nc, *args)
    r = run_bass_kernel_spmd(nc, [given], core_ids=[0])
    return r.results[0]["out"]
```

```python
from contextlib import ExitStack

import concourse.bass as bass
from concourse import mybir

ALU = mybir.AluOpType
ACT = mybir.ActivationFunctionType
F32 = mybir.dt.float32
BF16 = mybir.dt.bfloat16
F32R = mybir.dt.float32r
I32 = mybir.dt.int32
U32 = mybir.dt.uint32
AX = mybir.AxisListType

P = 128
B, S, E = 4, 256, 256
T = B * S
NT = T // P
KC = E // P
H1, G1, D1 = 32, 8, 8
H2, D2, LAT = 16, 16, 64
HG = 4
NX, F = 8, 176
FT = (NX + 1) * F
FC = (FT + P - 1) // P
FCR = NX * F // P
FL = FT - (FC - 1) * P
DOWN_CUT = FC // 2
PARTS = 3
Q_PART = (0, 1, 2, 0, 1, 0)
K_PART = (0, 0, 0, 1, 1, 2)
STACK = len(Q_PART)
ROWS = P - PARTS
EPS = 1e-5
RSQRT_GUESS = 0x5F3759DF
NEWTON = 3
NBANK = 8
NPLACE = 3
N_WEIGHTS = 6
DOWN_LAG = 2
NHID = DOWN_LAG + 1
MISC = NBANK - 1
VBANK = 6

GROUPS = [(0, b, g) for b in range(B) for g in range(G1)] + [(1, b, g) for b in range(B) for g in range(H2 // HG)]
PER = (G1, H2 // HG)
DH = (D1, D2)
NK = (G1, H2)
NH = (H1, H2)


AFTER_PLACE = 4
WEIGHTS_FROM, WEIGHTS_EVERY = 15, 3
K2_AT = (4, 13, 21, 29)
NEG_AT, PASS2_AT = 2, 4
CHAIN = {
    (0, 0): (False, 0, 3, 10, 5, 7, 18, 20, 3),
    (0, 1): (False, 1, 3, 10, 5, 7, 18, 21, 3),
    (0, 2): (False, 1, 3, 9, 4, 7, 19, 21, 3),
    (0, 3): (True, 1, 3, 10, 5, 6, 12, 13, 3),
    (1, 0): (False, 0, 1, 8, 4, 6, 16, 18, 3),
    (1, 1): (False, 1, 3, 10, 5, 8, 19, 21, 3),
    (1, 2): (False, 4, 5, 12, 7, 9, 20, 21, 2),
    (1, 3): (False, 3, 4, 13, 6, 8, 18, 21, 2),
}


class Timeline:

    def __init__(self):
        self.pass1, self.pass2 = {}, {}
        self.items = {}
        self.chain = {}
        self.afterwards = {}
        for b in range(1, B):
            s = PER[0] * (b - 1) + 1
            for i, kind in enumerate(("q1", "k1", "v1")):
                self.add(s + i, 1, (kind, b))
            self.slow_split(s + 1, "q1", b)
            self.fast_split(s + 1, "k1", b)
            self.hook(s + 3, "stack_first", b)
        for b in range(B):
            s = K2_AT[b]
            self.add(s, 1, ("k2", b))
            self.slow_split(s + 1, "k2", b)
            self.add(s + 1, 1, ("v2", b))
        for i in range(N_WEIGHTS):
            self.hook(WEIGHTS_FROM + WEIGHTS_EVERY * i, "weights", i)
        ready = {(0, b): 0 for b in range(B)}
        ends = []
        p1 = p2 = -1
        n = 0
        while n < len(GROUPS):
            a, b, _ = GROUPS[n]
            if a == 1:
                ready[a, b] = max(ready[a, b], ends[B + b - NPLACE] + AFTER_PLACE)
            for i in range(PER[a]):
                p1 = max(p1 + 1, ready[a, b])
                self.pass1[p1] = n + i
            self.hook(p1 + 1, "negmax", a, b)
            self.items.setdefault((p1 + NEG_AT, 0), []).insert(0, ("neg", a, b))
            self.hook(p1 + NEG_AT, "stack_neg", a, b)
            p2 = max(p2, p1 + PASS2_AT - 1)
            for i in range(PER[a]):
                p2 = p2 + 1
                self.pass2[p2] = n + i
                if i % HG == HG - 1:
                    self.hook(p2 + 1, "put", n + i - HG + 1)
            ends.append(p2)
            s = p2 + 1
            i = B * a + b + NPLACE
            if B <= i < 2 * B:
                self.hook(s, "stack_k2", i - B)
            whole, fetch, scale, out, stats, norm, turn, project, stack = CHAIN[a, b]
            self.hook(s + fetch, "fetch", a, b)
            self.late(s + scale, "scale", a, b)
            self.add(s + out // 2, out % 2, ("out", a, b))
            if whole:
                self.hook(s + stats, "whole_norm", a + 1, b)
            else:
                self.late(s + stats, "stats", a + 1, b)
                self.hook(s + stats + 1, "newton", a + 1, b)
                self.late(s + norm, "norm", a + 1, b)
            self.add(s + turn // 2, turn % 2, ("turn", a + 1, b))
            self.add(s + project // 2, project % 2, ("q2" if a == 0 else "router", b))
            s += project // 2
            if a == 0:
                self.fast_split(s, "q2", b)
                ready[1, b] = s + stack
            else:
                self.late(s, "gates_a", b)
                self.late(s + 1, "gates_b", b)
                self.add(s + stack, 0, ("gates", b))
            n += PER[a]
        self.moe0 = max(p2 + 1, *(s for (s, _), its in self.items.items() if ("gates", 0) in its or ("gates", 1) in its))
        self.steps = self.moe0 + 2 * FC + DOWN_LAG

    def slow_split(self, s, *piece):
        self.hook(s, "rest", *piece)
        self.hook(s, "middle", *piece)
        self.hook(s + 1, "split", *piece)
        self.hook(s + 1, "store", *piece)

    def fast_split(self, s, *piece):
        self.late(s, "split", *piece)
        self.hook(s + 1, "store", *piece)

    def late(self, s, *what):
        self.afterwards.setdefault(s, []).append(what)

    def hook(self, s, *what):
        self.chain.setdefault(s, []).append(what)

    def add(self, s, slot, what):
        self.items.setdefault((s, slot), []).append(what)


def rsqrt_steps(eng, link, y, v, t, done=None):
    for k in range(NEWTON):
        link(eng.tensor_tensor(t, y, y, ALU.mult))
        link(eng.tensor_tensor(t, t, v, ALU.mult))
        link(eng.tensor_scalar(t, t, -0.5, 1.5, ALU.mult, ALU.add))
        last = eng.tensor_tensor(y, y, t, ALU.mult)
        if done is None or k < NEWTON - 1:
            link(last)
        else:
            last.then_inc(done, 1)


def decoder_kernel(nc, x, w_first, w_small, w_latent, w_up, w_down, w_down_last, out):
    line = Timeline()
    with ExitStack() as stack:
        def sb(name, shape, dt=F32):
            return stack.enter_context(nc.sbuf_tensor(name, shape, dt))

        def sem(name):
            return stack.enter_context(nc.semaphore(name))

        def sems(name, n):
            return [sem(f"{name}{i}") for i in range(n)]

        def scratch(name, shape, dt):
            return nc.dram_tensor(name, shape, dt, kind="Internal").ap()

        q_dram = [scratch(f"q_parts{a}", (PARTS, E, T), BF16) for a in range(2)]
        k_dram = [scratch(f"k_parts{a}", (STACK, NK[a] * DH[a], T), BF16) for a in range(2)]
        o_dram = [scratch(f"o_raw{a}", (B, DH[a] + 1, NH[a], S), F32) for a in range(2)]

        ps = stack.enter_context(nc.psum_tensor("ps", [P, NBANK, 512], F32))
        psb = ps[:, :, :].bitcast(BF16)

        res = sb("res", [P, NT, E])
        xnT = sb("xnT", [P, KC, T])
        stats = sb("stats", [P, 4, 2, 6])
        mean_var = sb("mean_var", [P, 4, 2, 2])
        var_eps = sb("var_eps", [P, 4, 2])
        rstd = sb("rstd", [P, 4, 2])
        newton = sb("newton", [P, 4, 2])
        w_small_s = sb("w_small_s", [P, KC, 3 * E + NX])
        wo_s = [w_small_s[:, :, 0:E], w_small_s[:, :, 2 * E:3 * E]]
        wq2 = w_small_s[:, :, E:2 * E]
        gate_T = w_small_s[:, :, 3 * E:3 * E + NX]
        up_s = sb("up_s", [P, 2, KC, FT])
        down = sb("down", [P, FC, E])
        NQKV = E + 2 * G1 * D1
        shared = sb("shared", [P, 5 * 512])
        wqkv = shared[:, 0:KC * NQKV].rearrange("p (c n) -> p c n", c=KC)
        latent = shared[0:LAT, KC * NQKV:KC * NQKV + T + 2 * E]
        wkv2 = latent[:, 0:2 * E]
        ctx_T = latent[:, 2 * E:2 * E + T]
        silu = shared[:, 0:2 * 512].rearrange("p (c n) -> p c n", c=2)
        hidden = shared[:, 2 * 512:4 * 512].rearrange("p (c n) -> p c n", c=2)
        mid = shared[:, 4 * 512:5 * 512]
        ident = sb("ident", [P, P])
        identb = sb("identb", [P, P], BF16)
        mask = sb("mask", [P, P], BF16)
        ones = sb("ones", [PARTS, S], BF16)
        select = sb("select", [PARTS * NX, NX * F], BF16)
        number = sb("number", [P, NX])
        with nc.sbuf_tensor("q_stack", [P, H1, NPLACE, S], BF16) as q_stack:
            pass
        with ExitStack() as later_use:
            def sb_later(name, shape):
                return later_use.enter_context(nc.sbuf_tensor(name, shape, F32R))

            x_half = [sb_later(f"x_half{i}", [P, KC, T]) for i in range(2)]
            up_half = [sb_later(f"up_half{i}", [P, 2, 2, KC, P]) for i in range(2)]
            down_half = [sb_later(f"down_half{i}", [P, 2, E]) for i in range(2)]
            hid_half = [sb_later(f"hid_half{i}", [P, NHID, 512]) for i in range(2)]
        sb("place_of_both", [P, H1 * NPLACE * S], BF16)
        k_stack = sb("k_stack", [P, H2, NPLACE, S], BF16)
        NPB = 2
        exact = sb("exact", [P, NPB, KC, S])
        parts = sb("parts", [P, NPB, PARTS, KC, S], BF16)
        v_s = [sb("v0", [P, NT, G1 * (D1 + 1) + 32]), sb("v1", [P, NT, H2 * (D2 + 1) + 32])]
        v_head = [v_s[a][:, :, 0:(G1, H2)[a] * (DH[a] + 1)].rearrange("p t (h d) -> p t h d", d=DH[a] + 1)
                  for a in range(2)]
        rowmax = sb("rowmax", [P, 2, 2 * H1])
        neg_rest = sb("neg_rest", [P, 2, 2 * H1])
        neg_parts = sb("neg_parts", [P, 2, PARTS, 2 * H1], BF16)
        neg_T = sb("neg_T", [H1, 2, PARTS, S], BF16)
        probs = sb("probs", [P, 2, 3, 512])
        xn_first = probs[:, :, :, :].rearrange("p a b c -> p (a b c)")[:, 0:B * 2 * E]\
            .rearrange("p (b h e) -> p b h e", b=B, h=2)
        xn = sb("xn", [P, 2, E])
        NRAW = 2 * HG
        o_raw = sb("o_raw", [P, NRAW, S])
        o_T = sb("o_T", [P, KC, S])
        r_T = sb("r_T", [P, S])
        logits = sb("logits", [P, 2, NX])
        shifted = sb("shifted", [P, 2, NX])
        expd = sb("expd", [P, 2, NX])
        prob = sb("prob", [P, 2, NX])
        small = sb("small", [P, 4, 2])
        top = sb("top", [P, 2, 8])
        top_at = sb("top_at", [P, 2, 8], U32)
        top_w = sb("top_w", [P, 2, 2])
        top_f = sb("top_f", [P, 2, 2])
        gate0 = sb("gate0", [P, 2, NX])
        gate1 = sb("gate1", [P, 2, NX])
        gate_parts = sb("gate_parts", [P, 2, PARTS, NX], BF16)
        gates_T = sb("gates_T", [PARTS * NX, T], BF16)
        s_x = sems("x_loaded", B)
        s_wqkv = sem("wqkv_loaded")
        s_small = sem("small_weights_loaded")
        s_latent = sem("latent_loaded")
        s_moe = sem("expert_weights_loaded")
        s_ones = sems("ones_rows_stored", H2 // G1)
        s_kzero = sem("k_rows_zeroed")
        s_qzero = sem("q_rows_zeroed")
        s_sel = sem("select_copied")
        s_ident = sem("identity_made")
        s_mask = sem("mask_made")
        s_onesrow = sem("ones_made")
        s_const = sem("constants_made")
        s_xn = sem("xn_done")
        s_mm = sem("item_in_psum")
        s_item = sem("item_copied_out")
        s_split = [sem("split_by_vector"), sem("split_by_pool")]
        s_rest = sem("rest_of_piece")
        s_middle = sem("middle_of_piece")
        s_stats = sem("variance_and_guess")
        s_rstd = sem("rstd_done")
        s_parts_out = sems("parts_stored", NPB)
        s_qst = [sems("q0_stacked", B), sems("q1_stacked", B)]
        s_kst = [sems("k0_stacked", B), sems("k1_stacked", B)]
        s_p1 = sem("scores_for_max")
        s_max = sem("maxima_done")
        s_neg = sem("negmax_parts")
        s_nst = [sems("neg0_stacked", B), sems("neg1_stacked", B)]
        s_p2 = sem("scores_for_exp")
        s_exp = sem("exp_done")
        s_keep = sem("masked")
        s_pv = sem("pv_done")
        s_raw = sem("o_raw_copied")
        s_put = sems("o_raw_stored", len(GROUPS) // HG)
        s_vones = sem("v_ones_set")
        s_oT = sem("o_T_loaded")
        s_rT = sem("sums_loaded")
        s_scaled = sem("oT_scaled")
        s_ga = sem("logits_shifted")
        s_gexp = sem("router_exp")
        s_gp = sem("gate_parts_done")
        s_g = sem("gate_proj")
        s_u = sem("up_proj")
        s_e = sem("gates_spread")
        s_silu = sem("silu_done")
        s_h = sem("hidden_done")
        s_down = sem("down_done")
        s_xhi = sem("x_first_halves")
        s_xlo = sem("x_second_halves")
        s_uphi = sem("up_first_halves")
        s_uplo = sem("up_second_halves")
        s_dnhi = sem("down_first_halves")
        s_dnlo = sem("down_second_halves")
        s_hid = sem("hidden_rows")
        s_hidhi = sem("hidden_first_halves")
        s_y = sem("result_done")
        s_out = sem("result_stored")
        seq_v = sem("vector_sequence")
        seq_p = sem("pool_sequence")

        def linker(eng, s):
            count = [0]

            def link(ins, n=1):
                count[0] += n
                ins.then_inc(s, n)
                eng.wait_ge(s, count[0])
                return ins

            return link

        first = [("turn", 0, 0), ("q1", 0), ("k1", 0), ("v1", 0)] + [("turn", 0, b) for b in range(1, B)]
        later = []
        for s in range(line.steps):
            later += line.items.get((s, 0), []) + line.items.get((s, 1), [])
        number_of = {it: k for k, it in enumerate(first + later)}
        def by_pool(piece):
            return piece[0] == "k2" or (piece[0] == "q1" and piece[1] > 0)

        pieces = [it for it in first + later if it[0] in ("q1", "k1", "q2", "k2")]
        piece_of = {p: i for i, p in enumerate(pieces)}
        splitter = [1 if by_pool(p) else 0 for p in pieces]
        split_no = [splitter[:i + 1].count(splitter[i]) for i in range(len(pieces))]
        n_stores = {"q1": KC, "q2": KC, "k1": PARTS, "k2": PARTS * KC}

        def stores_until(i):
            return sum(n_stores[pieces[k][0]] for k in range(i % NPB, i + 1, NPB))

        def chains(*kinds):
            found = [w[1:] for s in range(line.steps) for w in line.chain.get(s, []) + line.afterwards.get(s, [])
                     if w[0] in kinds]
            return {w: i for i, w in enumerate(found)}

        order = {k: chains(k) for k in ("negmax", "scale", "gates_a", "gates_b")}
        norm_of = {(0, b): b for b in range(B)} | {w: B + i for w, i in chains("norm", "whole_norm").items()}
        newton_of = chains("newton")
        NORM_ORDER = {k: ab for ab, k in norm_of.items()}
        last_group = {GROUPS[n][:2]: n for n in range(len(GROUPS))}

        def head_slots(n):
            a, _, g = GROUPS[n]
            return slice(g, H1, G1) if a == 0 else slice(HG * g, HG * g + HG)

        def place_of(a, b):
            return (B * a + b) % NPLACE

        def x_views(hf):
            tok = slice(512 * hf, 512 * hf + 512)
            return x_half[0][:, :, tok], x_half[1][:, :, tok], xnT[:, :, tok]

        def up_views(n):
            fc = n % FC
            m = FL if fc == FC - 1 else P
            return *(u[:, n % 2, :, :, 0:m] for u in up_half), up_s[:, :, :, P * fc:P * fc + m]

        def down_views(n):
            fc = n % FC
            r = FL if fc == FC - 1 else P
            return *(d[0:r, n % 2, :] for d in down_half), down[0:r, fc, :]

        def hid_views(n):
            r = FL if n % FC == FC - 1 else P
            return *(h[0:r, n % NHID, :] for h in hid_half), hidden[0:r, n % 2, :]

        def splits_x(c):
            return {-1: 0, FC - 1: 1}.get(c)

        block = stack.enter_context(nc.Block())

        @block.sync
        def _(sp):
            def load_x(b):
                sp.dma_start(res[:, 2 * b:2 * b + 2, :], x[b].rearrange("(h p) e -> p h e", p=P)).then_inc(s_x[b], 16)

            load_x(0)
            sp.dma_start(wqkv[:, :, :], w_first).then_inc(s_wqkv, 16)
            for b in range(1, B):
                load_x(b)
            sp.dma_start(latent[:, :], w_latent).then_inc(s_latent, 16)
            sp.dma_start(w_small_s[:, :, :], w_small).then_inc(s_small, 16)
            def store_ones(k):
                sp.wait_ge(s_onesrow, 1)
                sp.wait_ge(s_kzero, k + 1)
                sp.dma_start(k_stack[ROWS:P, G1 * k:G1 * k + G1, :, :].rearrange("p h c t -> p (h c) t"),
                             ones[:, None, :].to_broadcast([PARTS, G1 * NPLACE, S])).then_inc(s_ones[k], 16)

            store_ones(0)

            def store_parts(piece):
                kind, b = piece
                i = piece_of[piece]
                a = 0 if kind in ("q1", "k1") else 1
                dram = (q_dram if kind[0] == "q" else k_dram)[a]
                rows = min(P, dram.shape[1])
                buf = i % NPB
                sp.wait_ge(s_split[splitter[i]], split_no[i])
                for c in range(dram.shape[1] // rows):
                    dst = dram[:, rows * c:rows * c + rows, b * S:b * S + S].rearrange("j r t -> r j t")
                    if kind[0] == "q":
                        sp.dma_start(dst, parts[:, buf, :, c, :]).then_inc(s_parts_out[buf], 16)
                        continue
                    for part in range(PARTS):
                        slots = [j for j in range(STACK) if K_PART[j] == part]
                        sp.dma_start(dst[:, slots[0]:slots[-1] + 1, :],
                                     parts[0:rows, buf, part, c, :][:, None, :].to_broadcast([rows, len(slots), S]))\
                          .then_inc(s_parts_out[buf], 16)

            def stored(piece):
                i = piece_of[piece]
                sp.wait_ge(s_parts_out[i % NPB], 16 * stores_until(i))

            def place_free(a, b):
                i = B * a + b - NPLACE
                if i >= 0:
                    sp.wait_ge(s_p2, 2 * last_group[i // B, i % B] + 2)

            def load_q(a, b):
                d = DH[a]
                tok = slice(b * S, b * S + S)
                r = 0
                for n in range(PARTS, 0, -1):
                    sp.dma_start(q_stack[r:r + n * d, 0:NH[a], place_of(a, b), :],
                                 q_dram[a][0:n, :, tok].rearrange("j (d h) t -> (j d) h t", d=d))\
                      .then_inc(s_qst[a][b], 16)
                    r += n * d

            def load_k(a, b):
                d = DH[a]
                sp.dma_start(k_stack[0:STACK * d, 0:NK[a], place_of(a, b), :],
                             k_dram[a][:, :, b * S:b * S + S].rearrange("j (d h) t -> (j d) h t", d=d))\
                  .then_inc(s_kst[a][b], 16)

            def stack_first(b):
                stored(("q1", b))
                place_free(0, b)
                sp.wait_ge(s_qzero, min(b + 1, NPLACE))
                load_q(0, b)
                stored(("k1", b))
                sp.wait_ge(s_kzero, 1)
                load_k(0, b)

            store_parts(("q1", 0))
            store_parts(("k1", 0))
            stack_first(0)
            store_ones(1)
            for s in range(line.steps):
                for what, *arg in line.chain.get(s, []):
                    if what == "store":
                        store_parts(tuple(arg))
                        if arg[0] == "q2":
                            b = arg[1]
                            stored(("q2", b))
                            place_free(1, b)
                            load_q(1, b)
                    if what == "weights":
                        i, = arg
                        if i < 2 * KC:
                            w, c = divmod(i, KC)
                            sp.dma_start(up_s[:, w, c, :], w_up[:, w, c, :]).then_inc(s_moe, 16)
                        elif i < 2 * KC + 1:
                            sp.dma_start(down[:, 0:DOWN_CUT, :], w_down[:, 0:DOWN_CUT, :]).then_inc(s_moe, 16)
                            sp.wait_ge(s_const, 1)
                            for p in range(1, PARTS):
                                sp.dma_start(select[NX * p:NX * p + NX, :], select[0:NX, :]).then_inc(s_sel, 16)
                        else:
                            sp.dma_start(down[:, DOWN_CUT:FC - 1, :], w_down[:, DOWN_CUT:FC - 1, :])\
                              .then_inc(s_moe, 16)
                            sp.dma_start(down[0:FL, FC - 1, :], w_down_last).then_inc(s_moe, 16)
                    if what == "stack_first":
                        stack_first(*arg)
                    if what == "stack_k2":
                        b, = arg
                        stored(("k2", b))
                        place_free(1, b)
                        load_k(1, b)
                    if what == "put":
                        n0, = arg
                        a, b, g0 = GROUPS[n0]
                        d = DH[a]
                        sp.wait_ge(s_raw, n0 + HG)
                        for j in range(HG):
                            h = NH[a] // HG * j + g0
                            sp.dma_start(o_dram[a][b, :, h:h + HG, :],
                                         o_raw[32 * j:32 * j + d + 1, n0 % NRAW:n0 % NRAW + HG, :])\
                              .then_inc(s_put[n0 // HG], 16)
                    if what == "stack_neg":
                        a, b = arg
                        i = order["negmax"][a, b]
                        sp.wait_ge(s_item, number_of["neg", a, b] + 1)
                        for p in range(PARTS):
                            sp.dma_start(q_stack[ROWS + p:ROWS + p + 1, 0:NH[a], place_of(a, b), :],
                                         neg_T[0:NH[a], i % 2, p, :]).then_inc(s_nst[a][b], 16)
                    if what == "fetch":
                        a, b = arg
                        i = order["scale"][a, b]
                        d = DH[a]
                        for n0 in range(last_group[a, b] + 1 - PER[a], last_group[a, b], HG):
                            sp.wait_ge(s_put[n0 // HG], 16 * HG)
                        if i >= 1:
                            sp.wait_ge(s_scaled, i)
                            sp.wait_ge(s_mm, number_of["out", (i - 1) // B, (i - 1) % B] + 1)
                        sp.dma_start(r_T[:, :], o_dram[a][b, d:d + 1].to_broadcast([d // KC, NH[a], S]))\
                          .then_inc(s_rT, 16)
                        sp.dma_start(o_T[:, :, :], o_dram[a][b, 0:d].rearrange("(c d) h t -> (d h) c t", c=KC))\
                          .then_inc(s_oT, 16)
                if s - line.moe0 in (FC + DOWN_LAG - 1, 2 * FC + DOWN_LAG - 1):
                    hf = (s - line.moe0) // FC - 1
                    for k in range(2):
                        sp.wait_ge(s_y, 2 * hf + k + 1)
                        sp.dma_start(out[2 * hf + k].rearrange("(h p) e -> p h e", p=P),
                                     res[:, 4 * hf + 2 * k:4 * hf + 2 * k + 2, :]).then_inc(s_out, 16)
            sp.wait_ge(s_out, 16 * B)

        def piece_views(piece):
            i = piece_of[piece]
            rows, chunks = (G1 * D1, 1) if piece[0] == "k1" else (P, KC)
            return exact[0:rows, i % NPB, 0:chunks, :], *(parts[0:rows, i % NPB, j, 0:chunks, :]
                                                          for j in range(PARTS))

        def split(eng, link, piece):
            r, hi, mid_, lo = piece_views(piece)
            eng.wait_ge(s_item, number_of[piece] + 1)
            link(eng.tensor_tensor(r, r, hi, ALU.subtract))
            link(eng.tensor_copy(mid_, r))
            eng.tensor_tensor(lo, r, mid_, ALU.subtract).then_inc(s_split[0], 1)

        @block.gpsimd
        def _(pool):
            link = linker(pool, seq_p)
            link(pool.memset(ident[:, :], 0.0))
            pool.affine_select(out=ident[:, :], in_=ident[:, :], compare_op=ALU.not_equal, fill=1.0, base=0,
                               pattern=[[-1, P]], channel_multiplier=1).then_inc(s_ident, 1)
            pool.memset(ones[:, :], 1.0).then_inc(s_onesrow, 1)
            pool.memset(v_s[0][:, :, :], 1.0).then_inc(s_vones, 1)
            pool.memset(k_stack[:, 0:G1, :, :].bitcast(U32), 0).then_inc(s_kzero, 1)
            pool.memset(q_stack[:, :, 0, :].bitcast(U32), 0).then_inc(s_qzero, 1)
            pool.wait_ge(s_ident, 1)
            pool.tensor_copy(identb[:, :], ident[:, :])
            link(pool.memset(mask[:, :], 0.0))
            pool.affine_select(out=mask[:, :], in_=mask[:, :], compare_op=ALU.is_ge, fill=-1e30, base=0,
                               pattern=[[-1, P]], channel_multiplier=1).then_inc(s_mask, 1)
            for place in range(1, NPLACE):
                pool.memset(q_stack[:, :, place, :].bitcast(U32), 0).then_inc(s_qzero, 1)
                if place == 1:
                    pool.memset(k_stack[:, G1:H2, :, :].bitcast(U32), 0).then_inc(s_kzero, 1)
            pool.memset(v_s[1][:, :, :], 1.0).then_inc(s_vones, 1)
            for e in range(NX):
                pool.memset(number[:, e:e + 1], float(e))
            link(pool.memset(select[0:NX, :], 1.0))
            link(pool.affine_select(out=select[0:NX, :], in_=select[0:NX, :], compare_op=ALU.is_ge, fill=0.0,
                                    base=0, pattern=[[1, NX * F]], channel_multiplier=-F))
            pool.affine_select(out=select[0:NX, :], in_=select[0:NX, :], compare_op=ALU.is_ge, fill=0.0,
                               base=F - 1, pattern=[[-1, NX * F]], channel_multiplier=F).then_inc(s_const, 1)
            for s in range(line.steps):
                if s in line.pass2:
                    n = line.pass2[s]
                    for u, count in ((0, 2 * n + 1), (2, 2 * n + 2)):
                        blk = probs[:, n % 2, u, :].rearrange("p (h q) -> p h q", h=HG)
                        pool.wait_ge(s_exp, count)
                        pool.affine_select(out=blk, in_=blk, compare_op=ALU.is_ge, fill=0.0, base=0,
                                           pattern=[[0, HG], [1, P]], channel_multiplier=-1).then_inc(s_keep, 1)
                c = s - line.moe0
                if -1 <= c < 2 * FC - 1:
                    hi, lo, w = up_views(c + 1)
                    pool.wait_ge(s_uphi, c + 2)
                    if c >= 1:
                        pool.wait_ge(s_u, c)
                    pool.tensor_tensor(lo, w, hi, ALU.subtract).then_inc(s_uplo, 1)
                if 1 <= c <= 2 * FC:
                    hi, lo, w = down_views(c - 1)
                    pool.wait_ge(s_dnhi, c)
                    if c >= 3:
                        pool.wait_ge(s_down, c - 2)
                    pool.tensor_tensor(lo, w, hi, ALU.subtract).then_inc(s_dnlo, 1)
                for what, *arg in line.chain.get(s, []):
                    piece = tuple(arg)
                    if what == "rest":
                        r, hi, _, _ = piece_views(piece)
                        pool.wait_ge(s_item, number_of[piece] + 1)
                        pool.tensor_tensor(r, r, hi, ALU.subtract).then_inc(s_rest, 1)
                    if what == "split" and by_pool(piece):
                        r, _, mid_, lo = piece_views(piece)
                        pool.wait_ge(s_middle, split_no[piece_of[piece]])
                        pool.tensor_tensor(lo, r, mid_, ALU.subtract).then_inc(s_split[1], 1)
                    if what == "newton":
                        k = norm_of[piece]
                        pool.wait_ge(s_stats, newton_of[piece] + 1)
                        v, y, t = (z[:, k % 4, :] for z in (var_eps, rstd, newton))
                        rsqrt_steps(pool, link, y, v, t, s_rstd)

        @block.scalar
        def _(act):
            def copy(dst, src, scale=None):
                return act.activation(dst, src, ACT.Copy, scale=scale) if scale else act.copy(dst, src)

            def copy_item(it):
                if it[0] == "out":
                    return
                k = number_of[it]
                bank = k % NBANK if k < len(first) else MISC
                act.wait_ge(s_mm, k + 1)
                kind = it[0]
                if kind == "turn":
                    b = it[2]
                    last = copy(xnT[:, :, b * S:b * S + S], ps[:, bank, :].rearrange("p (c t) -> p c t", c=KC))
                elif kind in ("q1", "q2", "k1", "k2"):
                    i = piece_of[it]
                    buf = i % NPB
                    rows, chunks = (G1 * D1, 1) if kind == "k1" else (P, KC)
                    scale = {"q1": D1 ** -0.5, "q2": D2 ** -0.5}.get(kind)
                    if i >= NPB:
                        j = i - NPB
                        act.wait_ge(s_split[splitter[j]], split_no[j])
                        act.wait_ge(s_parts_out[buf], 16 * stores_until(j))
                    src = ps[0:rows, bank, 0:chunks * S].rearrange("p (c t) -> p c t", c=chunks)
                    copy(exact[0:rows, buf, 0:chunks, :], src, scale)
                    last = copy(parts[0:rows, buf, 0, 0:chunks, :], src, scale)
                elif kind == "v1":
                    b = it[1]
                    act.wait_ge(s_vones, 1)
                    last = copy(v_head[0][:, 2 * b:2 * b + 2, :, 0:D1],
                                ps[:, bank, 0:2 * G1 * D1].rearrange("p (t g d) -> p t g d", t=2, d=D1))
                elif kind == "v2":
                    b = it[1]
                    act.wait_ge(s_vones, 2)
                    last = copy(v_head[1][:, 2 * b:2 * b + 2, :, 0:D2],
                                ps[:, bank, :].rearrange("p (t h d) -> p t h d", t=2, d=D2))
                elif kind == "neg":
                    a, b = it[1:]
                    i = order["negmax"][a, b]
                    if i >= 2:
                        a0, b0 = (i - 2) // B, (i - 2) % B
                        act.wait_ge(s_nst[a0][b0], 16 * PARTS)
                    last = copy(neg_T[0:NH[a], i % 2, :, :],
                                psb[0:NH[a], bank, 0:PARTS * S].rearrange("p (j t) -> p j t", j=PARTS))
                elif kind == "router":
                    last = copy(logits[:, :, :], ps[:, bank, 0:2 * NX].rearrange("p (t e) -> p t e", t=2))
                else:
                    b = it[1]
                    last = copy(gates_T[:, b * S:b * S + S], psb[0:PARTS * NX, bank, 0:S])
                last.then_inc(s_item, 1)

            for it in first:
                copy_item(it)
            for s in range(line.steps):
                for it in line.items.get((s, 0), []):
                    copy_item(it)
                n = line.pass2.get(s)
                if n is not None:
                    act.wait_ge(s_p2, 2 * n + 1)
                    if n >= 2:
                        act.wait_ge(s_pv, n - 1)
                    act.activation(probs[:, n % 2, 0, :], ps[:, 3, :], ACT.Exp).then_inc(s_exp, 1)
                for it in line.items.get((s, 1), []):
                    copy_item(it)
                if n is not None:
                    act.wait_ge(s_p2, 2 * n + 2)
                    act.activation(probs[:, n % 2, 1:3, :], ps[:, 4:6, :], ACT.Exp).then_inc(s_exp, 1)
                before = line.pass2.get(s - 1)
                if before is not None:
                    act.wait_ge(s_pv, before + 1)
                    if before >= NRAW:
                        act.wait_ge(s_put[(before - NRAW) // HG], 16 * HG)
                    copy(o_raw[:, before % NRAW, :], ps[:, VBANK, 0:S]).then_inc(s_raw, 1)
                c = s - line.moe0
                if 0 <= c < 2 * FC:
                    rows = FL if c % FC == FC - 1 else P
                    act.wait_ge(s_g, c + 1)
                    if c >= 2:
                        act.wait_ge(s_hid, c - 1)
                    act.activation(silu[0:rows, c % 2, :], ps[0:rows, c % 2, :], ACT.Silu).then_inc(s_silu, 1)
                if splits_x(c) is not None:
                    hf = splits_x(c)
                    act.wait_ge(s_p2, 2 * len(GROUPS))
                    act.wait_ge(s_item, number_of["turn", 2, 2 * hf + 1] + 1)
                    hi, _, x_ = x_views(hf)
                    copy(hi, x_).then_inc(s_xhi, 1)
                if -1 <= c < 2 * FC - 1:
                    hi, _, w = up_views(c + 1)
                    if c == -1:
                        act.wait_ge(s_moe, 16 * (N_WEIGHTS + 1))
                    if c >= 1:
                        act.wait_ge(s_u, c)
                        act.wait_ge(s_uplo, c)
                    copy(hi, w).then_inc(s_uphi, 1)
                if 1 <= c <= 2 * FC:
                    hi, _, w = down_views(c - 1)
                    if c >= 3:
                        act.wait_ge(s_down, c - 2)
                        act.wait_ge(s_dnlo, c - 2)
                    copy(hi, w).then_inc(s_dnhi, 1)
                if 0 <= c < 2 * FC:
                    hi, _, h_ = hid_views(c)
                    act.wait_ge(s_hid, c + 1)
                    if c >= NHID:
                        act.wait_ge(s_down, c - NHID + 1)
                        act.wait_ge(s_h, c - NHID + 1)
                    copy(hi, h_).then_inc(s_hidhi, 1)
                for what, *arg in line.chain.get(s, []):
                    if what == "middle":
                        piece = tuple(arg)
                        r, _, mid_, _ = piece_views(piece)
                        act.wait_ge(s_rest, split_no[piece_of[piece]])
                        copy(mid_, r).then_inc(s_middle, 1)
                for what, *arg in line.afterwards.get(s, []):
                    if what == "gates_a":
                        act.wait_ge(s_ga, order["gates_a"][tuple(arg)] + 1)
                        act.activation(expd[:, :, :], shifted[:, :, :], ACT.Exp).then_inc(s_gexp, 1)

        @block.vector
        def _(dve):
            link = linker(dve, seq_v)

            def variance(k, b):
                for h in range(2):
                    last = dve.bn_stats(stats[:, k % 4, h, :], res[:, 2 * b + h, :])
                link(last)
                for h in range(2):
                    last = dve.bn_aggr(mean_var[:, k % 4, h, :], stats[:, k % 4, h, :])
                link(last)
                link(dve.tensor_scalar(var_eps[:, k % 4, :], mean_var[:, k % 4, :, 1], EPS, None, ALU.add))

            def guess(v, y):
                link(dve.tensor_scalar(y.bitcast(I32), v.bitcast(I32), 1, None, ALU.arith_shift_right))
                return dve.tensor_scalar(y.bitcast(I32), y.bitcast(I32), -1, RSQRT_GUESS, ALU.mult, ALU.add)

            def rsqrt(k0, k1):
                v, y, t = (z[:, k0:k1, :] for z in (var_eps, rstd, newton))
                link(guess(v, y))
                rsqrt_steps(dve, link, y, v, t)

            def normed(k, b, dst):
                for h in range(2):
                    last = dve.tensor_scalar(dst[:, h, :], res[:, 2 * b + h, :], mean_var[:, k % 4, h, 0:1],
                                             rstd[:, k % 4, h:h + 1], ALU.subtract, ALU.mult)
                last.then_inc(s_xn, 1)

            def gates(b):
                i = order["gates_b"][b,]
                total, inv, den, rden = (small[:, k, :] for k in range(4))
                dve.wait_ge(s_gexp, i + 1)
                link(dve.tensor_reduce(total, expd[:, :, :], AX.X, ALU.add))
                link(dve.reciprocal(inv, total))
                link(dve.tensor_tensor(prob[:, :, :], expd[:, :, :], inv[:, :, None].to_broadcast([P, 2, NX]),
                                       ALU.mult))
                for h in range(2):
                    link(dve.max(top[:, h, :], prob[:, h, :]))
                for h in range(2):
                    link(dve.max_index(top_at[:, h, :], top[:, h, :], prob[:, h, :]))
                link(dve.tensor_copy(top_f[:, :, :], top_at[:, :, 0:2]))
                link(dve.tensor_tensor(den, top[:, :, 0], top[:, :, 1], ALU.add))
                link(dve.reciprocal(rden, den))
                link(dve.tensor_tensor(top_w[:, :, :], top[:, :, 0:2], rden[:, :, None].to_broadcast([P, 2, 2]),
                                       ALU.mult))
                for h in range(2):
                    for k, gate in enumerate((gate0, gate1)):
                        link(dve.tensor_scalar(gate[:, h, :], number[:, :], top_f[:, h, k:k + 1],
                                               top_w[:, h, k:k + 1], ALU.is_equal, ALU.mult))
                link(dve.tensor_tensor(gate0[:, :, :], gate0[:, :, :], gate1[:, :, :], ALU.add))
                hi, mi, lo = (gate_parts[:, :, j, :] for j in range(PARTS))
                link(dve.tensor_copy(hi, gate0[:, :, :]))
                link(dve.tensor_tensor(gate1[:, :, :], gate0[:, :, :], hi, ALU.subtract))
                link(dve.tensor_copy(mi, gate1[:, :, :]))
                dve.tensor_tensor(lo, gate1[:, :, :], mi, ALU.subtract).then_inc(s_gp, 1)

            def residual(a, b):
                i = number_of["out", a - 1, b]
                dve.wait_ge(s_mm, i + 1)
                tiles = res[:, 2 * b:2 * b + 2, :]
                dve.tensor_tensor(tiles, tiles, ps[:, MISC, :].rearrange("p (h e) -> p h e", h=2), ALU.add)\
                   .then_inc(s_item, 1)
                dve.wait_ge(s_item, i + 1)
                variance(norm_of[a, b], b)

            def norm_rows(a, b):
                k = norm_of[a, b]
                if k > B:
                    dve.wait_ge(s_mm, number_of[("turn",) + NORM_ORDER[k - 1]] + 1)
                normed(k, b, xn)

            dve.wait_ge(s_x[0], 16)
            variance(0, 0)
            rsqrt(0, 1)
            normed(0, 0, xn_first[:, 0])
            for b in range(1, B):
                dve.wait_ge(s_x[b], 16)
                variance(b, b)
            rsqrt(1, B)
            normed(1, 1, xn_first[:, 1])
            split(dve, link, ("q1", 0))
            split(dve, link, ("k1", 0))
            for b in range(2, B):
                normed(b, b, xn_first[:, b])

            for s in range(line.steps):
                for what, *arg in line.chain.get(s, []):
                    if what == "negmax":
                        a, b = arg
                        i = order["negmax"][a, b]
                        w = 2 * NH[a]
                        m, r = rowmax[:, i % 2, 0:w], neg_rest[:, i % 2, 0:w]
                        hi, mi, lo = (neg_parts[:, i % 2, j, 0:w] for j in range(PARTS))
                        dve.wait_ge(s_max, 2 * last_group[a, b] + 2)
                        link(dve.tensor_scalar(m, m, -1.0, None, ALU.mult))
                        link(dve.tensor_copy(hi, m))
                        link(dve.tensor_tensor(r, m, hi, ALU.subtract))
                        link(dve.tensor_copy(mi, r))
                        dve.tensor_tensor(lo, r, mi, ALU.subtract).then_inc(s_neg, 1)
                    if what == "whole_norm":
                        residual(*arg)
                        k = norm_of[tuple(arg)]
                        rsqrt(k % 4, k % 4 + 1)
                        norm_rows(*arg)
                n = line.pass1.get(s)
                if n is not None:
                    a, b, g = GROUPS[n]
                    i = order["negmax"][a, b]
                    m = rowmax[:, i % 2, :]
                    hs = head_slots(n)
                    dve.wait_ge(s_p1, 2 * n + 1)
                    dve.tensor_reduce(m[:, 0:NH[a]][:, hs], ps[:, 0, :].rearrange("p (h k) -> p h k", h=HG),
                                      AX.X, ALU.max).then_inc(s_max, 1)
                    dve.wait_ge(s_p1, 2 * n + 2)
                    dve.tensor_reduce(m[:, NH[a]:2 * NH[a]][:, hs],
                                      ps[:, 1:3, :].rearrange("p u (h k) -> p h u k", h=HG),
                                      AX.XY, ALU.max).then_inc(s_max, 1)
                for what, *arg in line.afterwards.get(s, []):
                    if what == "scale":
                        a, b = arg
                        i = order["scale"][a, b]
                        dve.wait_ge(s_rT, 16 * (i + 1))
                        link(dve.reciprocal(r_T[:, :], r_T[:, :]))
                        dve.wait_ge(s_oT, 16 * (i + 1))
                        dve.tensor_tensor(o_T[:, :, :], o_T[:, :, :], r_T[:, None, :].to_broadcast([P, KC, S]),
                                          ALU.mult).then_inc(s_scaled, 1)
                    if what == "split":
                        split(dve, link, tuple(arg))
                    if what == "stats":
                        residual(*arg)
                        k = norm_of[tuple(arg)]
                        guess(var_eps[:, k % 4, :], rstd[:, k % 4, :]).then_inc(s_stats, 1)
                    if what == "norm":
                        dve.wait_ge(s_rstd, newton_of[tuple(arg)] + 1)
                        norm_rows(*arg)
                    if what == "gates_a":
                        b, = arg
                        dve.wait_ge(s_item, number_of["router", b] + 1)
                        link(dve.tensor_reduce(small[:, 0, :], logits[:, :, :], AX.X, ALU.max))
                        dve.tensor_tensor(shifted[:, :, :], logits[:, :, :],
                                          small[:, 0, :, None].to_broadcast([P, 2, NX]), ALU.subtract)\
                            .then_inc(s_ga, 1)
                    if what == "gates_b":
                        gates(*arg)
                c = s - line.moe0
                if splits_x(c) is not None:
                    hi, lo, x_ = x_views(splits_x(c))
                    dve.wait_ge(s_xhi, splits_x(c) + 1)
                    dve.tensor_tensor(lo, x_, hi, ALU.subtract).then_inc(s_xlo, 1)
                if 0 <= c < 2 * FC:
                    fc = c % FC
                    rows = FL if fc == FC - 1 else P
                    hi, lo, h_ = hid_views(c)
                    dve.wait_ge(s_silu, c + 1)
                    dve.wait_ge(s_u, c + 1)
                    if c >= 1:
                        dve.wait_ge(s_hid, c)
                    if c >= 2:
                        dve.wait_ge(s_hidhi, c - 1)
                        dve.wait_ge(s_h, c - 1)
                    if fc < FCR:
                        link(dve.tensor_tensor(mid[:, :], silu[:, c % 2, :], ps[:, 2 + c % 2, :], ALU.mult))
                        dve.wait_ge(s_e, FCR * (c // FC) + fc + 1)
                        dve.tensor_tensor(h_, mid[:, :], ps[:, 4, :], ALU.mult).then_inc(s_hid, 1)
                    else:
                        dve.tensor_tensor(h_, silu[0:rows, c % 2, :], ps[0:rows, 2 + c % 2, :], ALU.mult)\
                           .then_inc(s_hid, 1)
                    dve.wait_ge(s_hidhi, c + 1)
                    if c >= NHID:
                        dve.wait_ge(s_down, c - NHID + 1)
                    dve.tensor_tensor(lo, h_, hi, ALU.subtract).then_inc(s_h, 1)
                if c in (FC + DOWN_LAG - 1, 2 * FC + DOWN_LAG - 1):
                    hf = c // FC - 1
                    dve.wait_ge(s_down, FC * (hf + 1))
                    for k in range(2):
                        tiles = res[:, 4 * hf + 2 * k:4 * hf + 2 * k + 2, :]
                        dve.tensor_tensor(tiles, ps[:, 5 + k, :].rearrange("p (t e) -> p t e", t=2), tiles,
                                          ALU.add).then_inc(s_y, 1)

        @block.tensor
        def _(pe):
            def mm(dst, lhsT, rhs, start=True, stop=True):
                return pe.matmul(dst, lhsT, rhs, start=start, stop=stop)

            def three_passes(dst, pairs, start=True, stop=True, **more):
                todo = [(a[i], b[j]) for a, b in pairs for i, j in ((0, 0), (0, 1), (1, 0))]
                for k, (a, b) in enumerate(todo):
                    last = pe.matmul(dst, a, b, start=start and k == 0, stop=stop and k == len(todo) - 1, **more)
                return last

            def item(it):
                k = number_of[it]
                bank = k % NBANK if k < len(first) else MISC
                if k >= len(first):
                    pe.wait_ge(s_item, k)
                elif k >= NBANK:
                    pe.wait_ge(s_item, k - NBANK + 1)
                kind = it[0]
                dst = ps[:, bank, :]
                if kind == "turn":
                    _, a, b = it
                    src = xn_first[:, b] if a == 0 else xn
                    pe.wait_ge(s_xn, norm_of[a, b] + 1)
                    for h in range(2):
                        for c in range(KC):
                            last = pe.transpose(dst[:, S * c + P * h:S * c + P * h + P], src[:, h, P * c:P * c + P],
                                                ident[:, :])
                elif kind in ("q1", "q2", "k1"):
                    b = it[1]
                    pe.wait_ge(s_item, number_of["turn", 1 if kind == "q2" else 0, b] + 1)
                    w, m, c0 = {"q1": (wqkv, P, 0), "k1": (wqkv, G1 * D1, E), "q2": (wq2, P, 0)}[kind]
                    for n in range(1 if kind == "k1" else KC):
                        for c in range(KC):
                            last = mm(dst[0:m, S * n:S * n + S], w[:, c, c0 + m * n:c0 + m * n + m],
                                      xnT[:, c, b * S:b * S + S], c == 0, c == KC - 1)
                elif kind == "v1":
                    b = it[1]
                    w = G1 * D1
                    for h in range(2):
                        t = 2 * b + h
                        for c in range(KC):
                            last = mm(dst[:, w * h:w * h + w], xnT[:, c, P * t:P * t + P],
                                      wqkv[:, c, E + w:E + 2 * w], c == 0, c == KC - 1)
                elif kind == "k2":
                    b = it[1]
                    for c in range(KC):
                        last = mm(dst[:, S * c:S * c + S], wkv2[:, P * c:P * c + P], ctx_T[:, b * S:b * S + S])
                elif kind == "v2":
                    b = it[1]
                    for h in range(2):
                        t = 2 * b + h
                        last = mm(dst[:, E * h:E * h + E], ctx_T[:, P * t:P * t + P], wkv2[:, E:2 * E])
                elif kind == "neg":
                    _, a, b = it
                    i = order["negmax"][a, b]
                    w = NH[a]
                    pe.wait_ge(s_neg, i + 1)
                    for j in range(PARTS):
                        for qb in range(2):
                            last = pe.transpose(psb[0:w, bank, S * j + P * qb:S * j + P * qb + P],
                                                neg_parts[:, i % 2, j, w * qb:w * qb + w], identb[:, :])
                elif kind == "out":
                    _, a, b = it
                    pe.wait_ge(s_scaled, order["scale"][a, b] + 1)
                    for h in range(2):
                        for c in range(KC):
                            last = mm(dst[:, E * h:E * h + E], o_T[:, c, P * h:P * h + P], wo_s[a][:, c, :],
                                      c == 0, c == KC - 1)
                elif kind == "router":
                    b = it[1]
                    pe.wait_ge(s_item, number_of["turn", 2, b] + 1)
                    for h in range(2):
                        t = 2 * b + h
                        for c in range(KC):
                            last = mm(dst[:, NX * h:NX * h + NX], xnT[:, c, P * t:P * t + P], gate_T[:, c, :],
                                      c == 0, c == KC - 1)
                else:
                    b = it[1]
                    pe.wait_ge(s_gp, order["gates_b"][b,] + 1)
                    for h in range(2):
                        last = pe.transpose(psb[0:PARTS * NX, bank, P * h:P * h + P],
                                            gate_parts[:, h, :, :].rearrange("p j e -> p (j e)"), identb[:, :])
                last.then_inc(s_mm, 1)

            def scores_max(n, blocks):
                a, b, g = GROUPS[n]
                rows = ROWS
                place = place_of(a, b)
                heads = range(H1)[head_slots(n)]
                for bank, qb, kb in blocks:
                    if qb == kb:
                        mm(ps[:, bank, :], identb[:, :], mask[:, None, :].to_broadcast([P, HG, P]), True, False)
                    for j, h in enumerate(heads):
                        last = mm(ps[:, bank, P * j:P * j + P],
                                  q_stack[0:rows, h, place, P * qb:P * qb + P],
                                  k_stack[0:rows, g if a == 0 else h, place, P * kb:P * kb + P],
                                  qb != kb, qb != kb or j == HG - 1)
                last.then_inc(s_p1, 1)

            def scores_exp(n, blocks):
                a, b, g = GROUPS[n]
                rows = P
                place = place_of(a, b)
                for bank, qb, kb in blocks:
                    q = q_stack[0:rows, head_slots(n), place, P * qb:P * qb + P]
                    if a == 0:
                        last = mm(ps[:, bank, :], k_stack[0:rows, g, place, P * kb:P * kb + P], q)
                        continue
                    for j, h in enumerate(range(H1)[head_slots(n)]):
                        last = mm(ps[:, bank, P * j:P * j + P], k_stack[0:rows, h, place, P * kb:P * kb + P],
                                  q_stack[0:rows, h, place, P * qb:P * qb + P])
                last.then_inc(s_p2, 1)

            def weigh(n):
                a, b, g = GROUPS[n]
                d = DH[a] + 1
                pe.wait_ge(s_keep, 2 * n + 2)
                if n >= 1:
                    pe.wait_ge(s_raw, n)
                heads = [g if a == 0 else h for h in range(H1)[head_slots(n)]]
                for kb in range(2):
                    for j, h in enumerate(heads):
                        last = mm(ps[32 * j:32 * j + 32, VBANK, P * kb:S],
                                  v_s[a][:, 2 * b + kb, d * h:d * h + 32],
                                  probs[:, n % 2, 2 * kb:2, P * j:P * j + P] if kb == 0 else
                                  probs[:, n % 2, 2, P * j:P * j + P], kb == 0, kb == 1)
                last.then_inc(s_pv, 1)

            pe.wait_ge(s_ident, 1)
            pe.wait_ge(s_wqkv, 16)
            for it in first:
                item(it)
            pe.wait_ge(s_item, len(first))
            pe.wait_ge(s_mask, 1)
            pe.wait_ge(s_ones[0], 16)
            pe.wait_ge(s_latent, 16)
            pe.wait_ge(s_small, 16)
            for s in range(line.steps):
                for it in line.items.get((s, 0), []):
                    item(it)
                m, n, before = line.pass1.get(s), line.pass2.get(s), line.pass2.get(s - 1)
                if m is not None:
                    a, b, g = GROUPS[m]
                    if g == 0:
                        pe.wait_ge(s_qst[a][b], 16 * PARTS)
                        pe.wait_ge(s_kst[a][b], 16)
                        if a == 1 and b == 0:
                            pe.wait_ge(s_ones[1], 16)
                    if m >= 1:
                        pe.wait_ge(s_max, 2 * m - 1)
                    scores_max(m, [(0, 0, 0)])
                if n is not None:
                    a, b, g = GROUPS[n]
                    if g == 0:
                        pe.wait_ge(s_nst[a][b], 16 * PARTS)
                    if n >= 1:
                        pe.wait_ge(s_exp, 2 * n - 1)
                    scores_exp(n, [(3, 0, 0)])
                for it in line.items.get((s, 1), []):
                    item(it)
                if m is not None:
                    if m >= 1:
                        pe.wait_ge(s_max, 2 * m)
                    scores_max(m, [(1, 1, 0), (2, 1, 1)])
                if n is not None:
                    if n >= 1:
                        pe.wait_ge(s_exp, 2 * n)
                    scores_exp(n, [(4, 1, 0), (5, 1, 1)])
                c = s - line.moe0
                if before is not None and c < 0:
                    weigh(before)
                if c == 0:
                    pe.wait_ge(s_exp, 2 * len(GROUPS))
                    pe.wait_ge(s_moe, 16 * (N_WEIGHTS + 1))
                    pe.wait_ge(s_sel, 16 * (PARTS - 1))
                if 0 <= c < 2 * FC:
                    hf, fc = divmod(c, FC)
                    m = FL if fc == FC - 1 else P
                    if fc == 0:
                        pe.wait_ge(s_item, number_of["gates", 2 * hf + 1] + 1)
                        pe.wait_ge(s_xlo, hf + 1)
                    xs = x_views(hf)
                    ws = up_views(c)
                    pe.wait_ge(s_uplo, c + 1)
                    if c >= 2:
                        pe.wait_ge(s_hid, c - 1)
                    for w, bank, done in ((0, 0, s_g), (1, 2, s_u)):
                        last = three_passes(ps[0:m, bank + c % 2, :],
                                            [([u[:, w, k, :] for u in ws[0:2]], [x_[:, k, :] for x_ in xs[0:2]])
                                             for k in range(KC)])
                        last.then_inc(done, 1)
                    if fc < FCR:
                        if c >= 1:
                            pe.wait_ge(s_hid, c)
                        mm(ps[:, 4, :], select[:, P * fc:P * fc + P], gates_T[:, 512 * hf:512 * hf + 512])\
                            .then_inc(s_e, 1)
                if before is not None and c == 0:
                    weigh(before)
                n = c - DOWN_LAG
                if n == 0:
                    pe.wait_ge(s_raw, len(GROUPS))
                if 0 <= n < 2 * FC:
                    hf, fc = divmod(n, FC)
                    ds, hs = down_views(n), hid_views(n)
                    pe.wait_ge(s_dnlo, n + 1)
                    pe.wait_ge(s_h, n + 1)
                    if fc == 0 and hf == 1:
                        pe.wait_ge(s_y, 2)
                    for t in range(4):
                        last = three_passes(ps[:, 5 + t // 2, E * (t % 2):E * (t % 2) + E],
                                            [([h[:, P * t:P * t + P] for h in hs[0:2]], ds[0:2])],
                                            fc == 0 and t % 2 == 0, fc == FC - 1, skip_group_check=True)
                    last.then_inc(s_down, 1)


def by_dim(w, heads):
    return w.reshape(w.shape[0], heads, -1).transpose(0, 2, 1).reshape(w.shape[0], -1)


def rows_on_partitions(w):
    return w.reshape(-1, P, w.shape[1]).transpose(1, 0, 2)


def kernel(x, ctx_512, L0_attn_Wq, L0_attn_Wk, L0_attn_Wv, L0_attn_Wo, L0_xattn_Wq, L0_xattn_Wkv_expand,
           L0_xattn_Wout, L0_ffn_gate_w, L0_ffn_w_gate, L0_ffn_w_up, L0_ffn_w_down, L0_ffn_sw_gate, L0_ffn_sw_up,
           L0_ffn_sw_down):
    import numpy as np
    import concourse.bacc as bacc
    from concourse.bass_utils import run_bass_kernel_spmd

    (x, ctx, wq, wk, wv, wo, xwq, xwkv, xwo, gate_w, w_gate, w_up, w_down, sw_gate, sw_up, sw_down) = (
        np.asarray(a) for a in (
            x, ctx_512, L0_attn_Wq, L0_attn_Wk, L0_attn_Wv, L0_attn_Wo, L0_xattn_Wq, L0_xattn_Wkv_expand,
            L0_xattn_Wout, L0_ffn_gate_w, L0_ffn_w_gate, L0_ffn_w_up, L0_ffn_w_down, L0_ffn_sw_gate, L0_ffn_sw_up,
            L0_ffn_sw_down))
    first = np.concatenate([by_dim(wq, H1), by_dim(wk, G1), wv], 1)
    strips = xwo.reshape(E, H2 // HG, HG, D2).transpose(0, 2, 1, 3).reshape(E, E)
    small = np.concatenate([by_dim(wo.T, H1).T, by_dim(xwq.T, H2), by_dim(strips, H2).T, gate_w.T], 1)
    latent = np.concatenate([by_dim(xwkv[0:E].T, H2), xwkv[E:2 * E].T, ctx.reshape(T, LAT).T], 1)
    ups = [np.concatenate([w.transpose(1, 0, 2).reshape(E, NX * F), one], 1)
           for w, one in ((w_gate, sw_gate), (w_up, sw_up))]
    downs = np.concatenate([w_down.reshape(NX * F, E), sw_down], 0)
    cut = (FC - 1) * P
    arrays = {
        "x": x,
        "w_first": rows_on_partitions(first),
        "w_small": rows_on_partitions(small),
        "w_latent": latent,
        "w_up": np.stack([rows_on_partitions(w) for w in ups], 1),
        "w_down": rows_on_partitions(downs[0:cut]),
        "w_down_last": downs[cut:FT],
    }
    nc = bacc.Bacc("TRN2", target_bir_lowering=False, num_devices=1)
    given, args = {}, []
    for name, a in arrays.items():
        given[f"in_{name}"] = a = np.ascontiguousarray(a)
        args.append(nc.dram_tensor(f"in_{name}", a.shape, mybir.dt.from_np(a.dtype), kind="ExternalInput").ap())
    args.append(nc.dram_tensor("out", (B, S, E), F32, kind="ExternalOutput").ap())
    decoder_kernel(nc, *args)
    r = run_bass_kernel_spmd(nc, [given], core_ids=[0])
    return r.results[0]["out"]
```
